# Optimizing a Trainium2 kernel written in Bass

```python
import numpy as np
import jax
import jax.numpy as jnp

def _softmax(x, axis=-1):
    return jax.nn.softmax(x, axis=axis)

def _gelu(x):
    return jax.nn.gelu(x, approximate=True)

def _silu(x):
    return jax.nn.silu(x)

def _sigmoid(x):
    return jax.nn.sigmoid(x)

def _layernorm(x, axis=-1, eps=1e-05):
    m = jnp.mean(x, axis=axis, keepdims=True)
    v = jnp.var(x, axis=axis, keepdims=True)
    return (x - m) / jnp.sqrt(v + eps)

def _scatter_add(tgt, idx, src, axis=0):
    return tgt.at[idx].add(src)

def _segment_sum(src, seg, n):
    return jax.ops.segment_sum(src, seg, n)
kernel_name = 'mk_vit_tower_d2_tok_img256_r4_5aeefe'

def setup_inputs(seed: int=0):
    np.random.seed(seed)
    _w = jnp.asarray

    def _rec_inputs():
        import jax
        import jax.numpy as jnp
        _rk = jax.random.key(seed)
        x = -0.0003702 + 0.999946 * jax.random.normal(jax.random.fold_in(_rk, 1), (128, 1, 84, 84), jnp.float32)
        return x
    x = _rec_inputs()

    def _L0_tok_setup():
        import jax, jax.numpy as jnp
        import numpy as np
        PH, PW = (64, 25)
        SH, SW = (64, 12)

        def _unfold(x, ph, pw, sh, sw):
            B, C, H, W = x.shape
            nh = (H - ph) // sh + 1
            nw = (W - pw) // sw + 1
            rows = jnp.arange(nh)[:, None] * sh + jnp.arange(ph)[None, :]
            cols = jnp.arange(nw)[:, None] * sw + jnp.arange(pw)[None, :]
            p = x[:, :, rows, :]
            p = p[:, :, :, :, cols]
            p = jnp.transpose(p, (0, 2, 4, 1, 3, 5))
            return p.reshape(B, nh * nw, C * ph * pw)
        key = jax.random.key(seed)
        kx, kw = jax.random.split(key, 2)
        x = jax.random.normal(kx, (64, 1, 64, 1000), dtype=jnp.float32)
        in_dim = 1 * PH * PW
        weight = jax.random.normal(kw, (in_dim, 64), dtype=jnp.float32) / np.sqrt(in_dim).astype(np.float32)
        bias = jnp.zeros((64,), dtype=jnp.float32)
        return {'x': x, 'weight': weight, 'bias': bias}
    _L0_tok_all = _L0_tok_setup()
    _L0_tok_in = {k: v for k, v in _L0_tok_all.items() if k in ('weight', 'bias')}
    del _L0_tok_all

    def _L0_attn_setup():
        import jax, jax.numpy as jnp
        import numpy as np
        B, N, D = (8, 512, 64)
        key = jax.random.key(seed)
        k1, k2, k3, k4 = jax.random.split(key, 4)
        s = D ** (-0.5)
        return {'x': jax.random.normal(k1, (B, N, D), dtype=jnp.float32), 'Wq': jax.random.normal(k2, (D, D), dtype=jnp.float32) * s, 'Wk': jax.random.normal(k3, (D, D), dtype=jnp.float32) * s, 'Wv': jax.random.normal(k4, (D, D), dtype=jnp.float32) * s}
    _L0_attn_all = _L0_attn_setup()
    _L0_attn_in = {k: v for k, v in _L0_attn_all.items() if k in ('Wq', 'Wk', 'Wv')}
    del _L0_attn_all

    def _L0_ffn_setup():
        import jax, jax.numpy as jnp
        import numpy as np
        B, S, H, NH, NE = (4, 256, 64, 4, 4)
        D = H // NH
        EPS = 1e-08

        def layernorm(x, g, b):
            m = jnp.mean(x, axis=-1, keepdims=True)
            v = jnp.mean((x - m) ** 2, axis=-1, keepdims=True)
            return (x - m) / jnp.sqrt(v + EPS) * g + b
        key = jax.random.key(seed)
        ks = jax.random.split(key, 18)
        sc = 0.05
        return {'x': jax.random.normal(ks[0], (B, S, H), jnp.float32), 'hl_w': jax.random.normal(ks[1], (NH, D, H), jnp.float32) * sc, 'hl_b': jax.random.normal(ks[2], (NH, D), jnp.float32) * sc, 'wq': jax.random.normal(ks[3], (NH, NE, D, D), jnp.float32) * sc, 'wk': jax.random.normal(ks[4], (NH, D, D), jnp.float32) * sc, 'wv': jax.random.normal(ks[5], (NH, D, D), jnp.float32) * sc, 'gate_w': jax.random.normal(ks[6], (NH, NE, NE * D), jnp.float32) * sc, 'gate_b': jax.random.normal(ks[7], (NH, NE), jnp.float32) * sc, 'ln_g': jnp.ones((D,), jnp.float32), 'ln_b': jnp.zeros((D,), jnp.float32), 'fc1_w': jax.random.normal(ks[8], (D, D), jnp.float32) * sc, 'fc1_b': jax.random.normal(ks[9], (D,), jnp.float32) * sc, 'fc2_w': jax.random.normal(ks[10], (D, D), jnp.float32) * sc, 'fc2_b': jax.random.normal(ks[11], (D,), jnp.float32) * sc, 'fnorm_g': jnp.ones((D,), jnp.float32), 'fnorm_b': jnp.zeros((D,), jnp.float32), 'fgate_w': jax.random.normal(ks[12], (NH, H), jnp.float32) * sc}
    _L0_ffn_all = _L0_ffn_setup()
    _L0_ffn_in = {k: v for k, v in _L0_ffn_all.items() if k in ('hl_w', 'hl_b', 'wq', 'wk', 'wv', 'gate_w', 'gate_b', 'ln_g', 'ln_b', 'fc1_w', 'fc1_b', 'fc2_w', 'fc2_b', 'fnorm_g', 'fnorm_b', 'fgate_w')}
    del _L0_ffn_all

    def _L1_attn_setup():
        import jax, jax.numpy as jnp
        import numpy as np
        EMBED_DIM = 64
        B, S = (4, 2048)
        key = jax.random.key(seed)
        ks = jax.random.split(key, 9)
        d = EMBED_DIM
        s = 1.0 / np.sqrt(d)
        return {'x': jax.random.normal(ks[0], (B, S, d), dtype=jnp.float32), 'Wq': jax.random.uniform(ks[1], (d, d), jnp.float32, -s, s), 'bq': jax.random.uniform(ks[2], (d,), jnp.float32, -s, s), 'Wk': jax.random.uniform(ks[3], (d, d), jnp.float32, -s, s), 'bk': jax.random.uniform(ks[4], (d,), jnp.float32, -s, s), 'Wv': jax.random.uniform(ks[5], (d, d), jnp.float32, -s, s), 'bv': jax.random.uniform(ks[6], (d,), jnp.float32, -s, s), 'Wo': jax.random.uniform(ks[7], (d, d), jnp.float32, -s, s), 'bo': jax.random.uniform(ks[8], (d,), jnp.float32, -s, s)}
    _L1_attn_all = _L1_attn_setup()
    _L1_attn_in = {k: v for k, v in _L1_attn_all.items() if k in ('Wq', 'bq', 'Wk', 'bk', 'Wv', 'bv', 'Wo', 'bo')}
    del _L1_attn_all

    def _L1_ffn_setup():
        import jax, jax.numpy as jnp
        import numpy as np
        C = 64
        HID = 256
        E = 8
        TEMP = 1.0
        key = jax.random.key(seed)
        ks = jax.random.split(key, 7)
        x = jax.random.normal(ks[0], (8, 4096, C), dtype=jnp.float32)
        W1 = jax.random.normal(ks[1], (C, HID), dtype=jnp.float32) * 0.02
        b1 = jnp.zeros((HID,), dtype=jnp.float32)
        Wg = jax.random.normal(ks[2], (HID, E), dtype=jnp.float32) * 0.02
        bg = jnp.zeros((E,), dtype=jnp.float32)
        Wd = jax.random.normal(ks[3], (E, HID, C), dtype=jnp.float32) * 0.02
        bd = jnp.zeros((E, C), dtype=jnp.float32)
        return {'x': x, 'W1': W1, 'b1': b1, 'Wg': Wg, 'bg': bg, 'Wd': Wd, 'bd': bd}
    _L1_ffn_all = _L1_ffn_setup()
    _L1_ffn_in = {k: v for k, v in _L1_ffn_all.items() if k in ('W1', 'b1', 'Wg', 'bg', 'Wd', 'bd')}
    del _L1_ffn_all
    return {'x': x, 'L0_tok_weight': _L0_tok_in['weight'], 'L0_tok_bias': _L0_tok_in['bias'], 'L0_attn_Wq': _L0_attn_in['Wq'], 'L0_attn_Wk': _L0_attn_in['Wk'], 'L0_attn_Wv': _L0_attn_in['Wv'], 'L0_ffn_hl_w': _L0_ffn_in['hl_w'], 'L0_ffn_hl_b': _L0_ffn_in['hl_b'], 'L0_ffn_wq': _L0_ffn_in['wq'], 'L0_ffn_wk': _L0_ffn_in['wk'], 'L0_ffn_wv': _L0_ffn_in['wv'], 'L0_ffn_gate_w': _L0_ffn_in['gate_w'], 'L0_ffn_gate_b': _L0_ffn_in['gate_b'], 'L0_ffn_ln_g': _L0_ffn_in['ln_g'], 'L0_ffn_ln_b': _L0_ffn_in['ln_b'], 'L0_ffn_fc1_w': _L0_ffn_in['fc1_w'], 'L0_ffn_fc1_b': _L0_ffn_in['fc1_b'], 'L0_ffn_fc2_w': _L0_ffn_in['fc2_w'], 'L0_ffn_fc2_b': _L0_ffn_in['fc2_b'], 'L0_ffn_fnorm_g': _L0_ffn_in['fnorm_g'], 'L0_ffn_fnorm_b': _L0_ffn_in['fnorm_b'], 'L0_ffn_fgate_w': _L0_ffn_in['fgate_w'], 'L1_attn_Wq': _L1_attn_in['Wq'], 'L1_attn_bq': _L1_attn_in['bq'], 'L1_attn_Wk': _L1_attn_in['Wk'], 'L1_attn_bk': _L1_attn_in['bk'], 'L1_attn_Wv': _L1_attn_in['Wv'], 'L1_attn_bv': _L1_attn_in['bv'], 'L1_attn_Wo': _L1_attn_in['Wo'], 'L1_attn_bo': _L1_attn_in['bo'], 'L1_ffn_W1': _L1_ffn_in['W1'], 'L1_ffn_b1': _L1_ffn_in['b1'], 'L1_ffn_Wg': _L1_ffn_in['Wg'], 'L1_ffn_bg': _L1_ffn_in['bg'], 'L1_ffn_Wd': _L1_ffn_in['Wd'], 'L1_ffn_bd': _L1_ffn_in['bd']}

def reference(x, L0_tok_weight, L0_tok_bias, L0_attn_Wq, L0_attn_Wk, L0_attn_Wv, L0_ffn_hl_w, L0_ffn_hl_b, L0_ffn_wq, L0_ffn_wk, L0_ffn_wv, L0_ffn_gate_w, L0_ffn_gate_b, L0_ffn_ln_g, L0_ffn_ln_b, L0_ffn_fc1_w, L0_ffn_fc1_b, L0_ffn_fc2_w, L0_ffn_fc2_b, L0_ffn_fnorm_g, L0_ffn_fnorm_b, L0_ffn_fgate_w, L1_attn_Wq, L1_attn_bq, L1_attn_Wk, L1_attn_bk, L1_attn_Wv, L1_attn_bv, L1_attn_Wo, L1_attn_bo, L1_ffn_W1, L1_ffn_b1, L1_ffn_Wg, L1_ffn_bg, L1_ffn_Wd, L1_ffn_bd):
    import jax
    import jax.numpy as jnp

    def _L0_tok_ref(x, weight, bias):
        import jax, jax.numpy as jnp
        import numpy as np
        PH, PW = (64, 25)
        SH, SW = (64, 12)

        def _unfold(x, ph, pw, sh, sw):
            B, C, H, W = x.shape
            nh = (H - ph) // sh + 1
            nw = (W - pw) // sw + 1
            rows = jnp.arange(nh)[:, None] * sh + jnp.arange(ph)[None, :]
            cols = jnp.arange(nw)[:, None] * sw + jnp.arange(pw)[None, :]
            p = x[:, :, rows, :]
            p = p[:, :, :, :, cols]
            p = jnp.transpose(p, (0, 2, 4, 1, 3, 5))
            return p.reshape(B, nh * nw, C * ph * pw)
        p = _unfold(x, PH, PW, SH, SW)
        return jax.nn.gelu(jnp.einsum('bnk,kd->bnd', p, weight) + bias, approximate=False)

    def _L0_attn_ref(x, Wq, Wk, Wv):
        import jax, jax.numpy as jnp
        import numpy as np
        B, N, D = (8, 512, 64)
        q = jnp.einsum('bnd,ed->bne', x, Wq)
        k = jnp.einsum('bnd,ed->bne', x, Wk)
        v = jnp.einsum('bnd,ed->bne', x, Wv)
        energy = jnp.einsum('bqd,bkd->bqk', q, k)
        scaling = jnp.asarray(x.shape[-1] ** (-0.5), x.dtype)
        att = jax.nn.softmax(energy, axis=-1) * scaling
        out = jnp.einsum('bqk,bkv->bqv', att, v)
        return out

    def _L0_ffn_ref(x, hl_w, hl_b, wq, wk, wv, gate_w, gate_b, ln_g, ln_b, fc1_w, fc1_b, fc2_w, fc2_b, fnorm_g, fnorm_b, fgate_w):
        import jax, jax.numpy as jnp
        import numpy as np
        B, S, H, NH, NE = (4, 256, 64, 4, 4)
        D = H // NH
        EPS = 1e-08

        def layernorm(x, g, b):
            m = jnp.mean(x, axis=-1, keepdims=True)
            v = jnp.mean((x - m) ** 2, axis=-1, keepdims=True)
            return (x - m) / jnp.sqrt(v + EPS) * g + b
        b, s, h = x.shape
        nh, d, _ = wk.shape
        ne = wq.shape[1]
        sx = jnp.einsum('bsh,ndh->bnsd', x, hl_w) + hl_b[None, :, None, :]
        pad = sx == 0
        q = jnp.einsum('bnsd,neod->bneso', sx, wq)
        k = jnp.einsum('bnsd,nod->bnso', sx, wk)
        v = jnp.einsum('bnsd,nod->bnso', sx, wv)
        causal = jnp.where(jnp.tril(jnp.ones((s, s), bool)), 0.0, -jnp.inf).astype(x.dtype)
        scores = jnp.einsum('bnesd,bntd->bnest', q, k) * d ** 0.5 + causal
        att = jax.nn.softmax(scores, axis=-1)
        qkv = jnp.einsum('bnest,bntd->bnesd', att, v)
        qkv = jnp.where(pad[:, :, None], 0.0, qkv)
        out = jnp.transpose(qkv, (0, 1, 3, 2, 4)).reshape(b, nh, s, ne * d)
        gs = jax.nn.softmax(jnp.einsum('bnsf,nef->bnse', out, gate_w) + gate_b[None, :, None, :], axis=-1)
        mixed = jnp.einsum('bnsed,bnse->bnsd', out.reshape(b, nh, s, ne, d), gs)
        resid = sx[jnp.arange(nh), jnp.arange(nh)]
        hn = layernorm(mixed + resid, ln_g, ln_b)
        f_n = jnp.transpose(hn, (0, 2, 1, 3)).reshape(b, s, h)
        fx = f_n.reshape(b, s, nh, d)
        pm = fx == 0
        hx = jnp.where(pm, 0.0, fx @ fc1_w.T + fc1_b)
        hx = jax.nn.relu(hx)
        hx = jnp.where(pm, 0.0, hx @ fc2_w.T + fc2_b)
        hx = layernorm(hx + fx, fnorm_g, fnorm_b)
        fout = hx.reshape(b, s, h)
        fg = jax.nn.softmax(fout @ fgate_w.T, axis=-1)
        return (fout.reshape(b, s, nh, d) * fg[..., None]).reshape(b, s, h)

    def _L1_attn_ref(x, Wq, bq, Wk, bk, Wv, bv, Wo, bo):
        import jax, jax.numpy as jnp
        import numpy as np
        EMBED_DIM = 64
        B, S = (4, 2048)
        d = x.shape[-1]
        scaling = d ** (-0.5)
        q = x @ Wq.T + bq
        k = x @ Wk.T + bk
        v = x @ Wv.T + bv
        scores = jnp.einsum('bsd,btd->bst', q, k) * scaling
        weights = jax.nn.softmax(scores, axis=-1)
        attn = jnp.einsum('bst,btd->bsd', weights, v)
        return attn @ Wo.T + bo

    def _L1_ffn_ref(x, W1, b1, Wg, bg, Wd, bd):
        import jax, jax.numpy as jnp
        import numpy as np
        C = 64
        HID = 256
        E = 8
        TEMP = 1.0
        orig_shape = x.shape
        xf = x.reshape(-1, orig_shape[-1])
        H = jax.nn.gelu(xf @ W1 + b1, approximate=False)
        probs = jax.nn.softmax((H @ Wg + bg) / TEMP, axis=-1)
        assign = jnp.argmax(probs, axis=-1)
        out = jnp.zeros_like(xf)
        for e in range(Wd.shape[0]):
            y = H @ Wd[e] + bd[e]
            sel = (assign == e)[:, None]
            out = out + jnp.where(sel, probs[:, e:e + 1] * y, 0.0)
        return out.reshape(orig_shape)
    h = _L0_tok_ref(x, L0_tok_weight, L0_tok_bias)
    h = h + _L0_attn_ref(_layernorm(h, axis=-1), L0_attn_Wq, L0_attn_Wk, L0_attn_Wv)
    h = h + _L0_ffn_ref(_layernorm(h, axis=-1), L0_ffn_hl_w, L0_ffn_hl_b, L0_ffn_wq, L0_ffn_wk, L0_ffn_wv, L0_ffn_gate_w, L0_ffn_gate_b, L0_ffn_ln_g, L0_ffn_ln_b, L0_ffn_fc1_w, L0_ffn_fc1_b, L0_ffn_fc2_w, L0_ffn_fc2_b, L0_ffn_fnorm_g, L0_ffn_fnorm_b, L0_ffn_fgate_w)
    h = h + _L1_attn_ref(_layernorm(h, axis=-1), L1_attn_Wq, L1_attn_bq, L1_attn_Wk, L1_attn_bk, L1_attn_Wv, L1_attn_bv, L1_attn_Wo, L1_attn_bo)
    h = h + _L1_ffn_ref(_layernorm(h, axis=-1), L1_ffn_W1, L1_ffn_b1, L1_ffn_Wg, L1_ffn_bg, L1_ffn_Wd, L1_ffn_bd)
    return h

_drawn_inputs = setup_inputs


def setup_inputs(seed=0):
    import zlib

    import numpy as np

    out = dict(_drawn_inputs(seed))
    spreads = {'L0_tok_bias': (0.0, 0.1),
     'L0_ffn_ln_g': (1.0, 0.2),
     'L0_ffn_ln_b': (0.0, 0.1),
     'L0_ffn_fnorm_g': (1.0, 0.2),
     'L0_ffn_fnorm_b': (0.0, 0.1),
     'L1_ffn_b1': (0.0, 0.61),
     'L1_ffn_bg': (0.0, 0.347),
     'L1_ffn_bd': (0.0, 0.401)}
    factors = {'L0_ffn_wq': 8.0,
     'L0_ffn_wk': 8.0,
     'L0_ffn_gate_w': 32.154,
     'L0_ffn_gate_b': 22.578,
     'L0_ffn_fc1_w': 4.679,
     'L0_ffn_fc1_b': 8.0,
     'L0_ffn_fc2_w': 3.914,
     'L1_attn_bq': 7.997,
     'L1_attn_bk': 64.0,
     'L1_ffn_W1': 3.65,
     'L1_ffn_Wg': 3.935,
     'L1_ffn_Wd': 8.0}
    for name, (base, spread) in spreads.items():
        noise = np.random.default_rng([zlib.crc32(name.encode()), seed]).standard_normal(out[name].shape)
        drawn = base * np.exp(spread * noise) if base else spread * noise
        out[name] = jnp.asarray(drawn.astype(out[name].dtype))
    for name, factor in factors.items():
        out[name] = (out[name] * factor).astype(out[name].dtype)
    return out
```

```python
import concourse.bass as bass
from concourse import mybir
from contextlib import ExitStack

B, S, D = 128, 5, 64
PH, PW, SW = 64, 25, 12
PAIRS = (SW * (S - 1) + PW + 1) // 2
STEPS = SW // 2
NH, DH, NE = 4, 16, 4
HID, E = 256, 8
KC = HID // 128
EPS, EPS_FFN = 1e-5, 1e-8
S0 = 3

W128 = {}
_at = 0
for _n, _c in (("ident", 128), ("wg", KC * E), ("gate_w", 2 * NE * NH), ("onehot", NH * 128), ("gate_b", NE * NH),
               ("ln_g", D), ("ln_b", D), ("fn_g", D), ("fn_b", D), ("fgate", NH * D), ("bg", E), ("first", E),
               ("bd", S * D)):
    W128[_n] = (_at, _c)
    _at += _c
N128 = _at
W65 = {}
_at = 0
for _n, _c in (("a0_q", D), ("a0_k", D), ("a0_v", D), ("hl_t", D + 1), ("hl", D), ("bd_v", D), ("bd_q", NE * D),
               ("bd_k", D), ("fc1", D), ("fc2", D), ("a1_q", D + 1), ("a1_k", D + 1), ("a1_v", D + 1),
               ("a1_o", D), ("w1", HID), ("bo", D), ("tok_b", S * D), ("ones", 128)):
    W65[_n] = (_at, _c)
    _at += _c
N65 = _at


def vit_tower_kernel(nc: bass.Bass, x: bass.AP, w_tok: bass.AP, w128: bass.AP, w65: bass.AP, wd: bass.AP,
                     out: bass.AP):
    fp32 = mybir.dt.float32
    ALU = mybir.AluOpType
    ACT = mybir.ActivationFunctionType
    X = mybir.AxisListType.X

    ctx = ExitStack()
    with ctx:
        def sb(name, shape):
            return ctx.enter_context(nc.sbuf_tensor(name, shape, fp32))

        def sem(name):
            return ctx.enter_context(nc.semaphore(name))

        x_sb = sb("x_sb", [128, PAIRS, B])
        wt_sb = sb("wt_sb", [128, D + STEPS * 2 * D])
        c128 = sb("c128", [128, N128])
        c65 = sb("c65", [65, N65])
        wd_sb = sb("wd_sb", [128, KC, E * D])
        t0q = sb("t0q", [D, 2 * D])
        t1q = sb("t1q", [D + 1, 2 * D + 1])
        mq = sb("mq", [D, NE * D])
        wf = sb("wf", [D + 1, 2 * D + NE * D])
        h = sb("h", [B, S, D])
        st = sb("st", [B, S, 6])
        ag = sb("ag", [B, S, 2])
        lnv = sb("lnv", [B, S])
        rstd = sb("rstd", [B, S])
        xc = sb("xc", [B, S, D])
        xa = sb("xa", [B, S, D + 1])
        aT = sb("aT", [D + 1, S, B])
        prod = sb("prod", [B, S * S * (D + 1)])
        sc = sb("sc", [B, S, S])
        mx = sb("mx", [B, S])
        p = sb("p", [B, S, S])
        sm = sb("sm", [B, S])
        att = sb("att", [B, S, D])
        sxv = sb("sxv", [B, S, 2 * D])
        fprod = sb("fprod", [B, S * NE * D])
        fs = sb("fs", [B, S, S, NE * NH])
        fm = sb("fm", [B, S, NE * NH])
        fp = sb("fp", [B, S, S, NE * NH])
        fr = sb("fr", [B, S, NE * NH])
        notpad = sb("notpad", [B, S, D])
        om = sb("om", [B, S, NE * D])
        omT = sb("omT", [128, 2 * S, B])
        lg = sb("lg", [B, S, NE * NH])
        gm = sb("gm", [B, S, NH])
        gs = sb("gs", [B, S, NE * NH])
        gr = sb("gr", [B, S, NH])
        y = sb("y", [B, S * NH, DH])
        yc = sb("yc", [B, S * NH, DH])
        sq = sb("sq", [B, S * NH, DH])
        s1 = sb("s1", [B, S * NH])
        s2 = sb("s2", [B, S * NH])
        ls = sb("ls", [B, S * NH])
        rs = sb("rs", [B, S * NH])
        f1 = sb("f1", [B, S, D + 1])
        m1 = sb("m1", [B, S, D])
        m1T = sb("m1T", [D, S, B])
        hT = sb("hT", [D + 1, S, B])
        fo = sb("fo", [B, S, D])
        fg = sb("fg", [B, S, NH])
        fgm = sb("fgm", [B, S])
        fge = sb("fge", [B, S, NH])
        fgr = sb("fgr", [B, S])
        gT = sb("gT", [128, KC, S, B])
        ml = sb("ml", [B, S, E])
        mm_ = sb("mm_", [B, S])
        me = sb("me", [B, S, E])
        mr = sb("mr", [B, S])
        mp = sb("mp", [B, S, E])
        mt = sb("mt", [B, S, E])
        wsel = sb("wsel", [B, S, E])
        wselT = sb("wselT", [S * E, B])
        yprod = sb("yprod", [B, 2, E * D])
        ysum = sb("ysum", [B, S, D])
        fin = sb("fin", [B, S, D])

        c_eps = sb("c_eps", [128, 1])
        c_epsf = sb("c_epsf", [128, 1])

        bank = [ctx.enter_context(nc.psum_tensor(f"bank{i}", [128, 512], fp32)) for i in range(8)]

        def c1(name):
            a, n = W128[name]
            return c128[:, a:a + n]

        def c6(name, rows=65):
            a, n = W65[name]
            return c65[0:rows, a:a + n]

        ident = c1("ident")

        wt_in = sem("wt_in")
        x_in = [sem(f"x_in{m}") for m in range(STEPS)]
        c128_in = sem("c128_in")
        c65_in = sem("c65_in")
        wd_in = sem("wd_in")
        tok_done = sem("tok_done")
        h_ready = sem("h_ready")
        var_ready = sem("var_ready")
        rstd_ready = sem("rstd_ready")
        xa_ready = sem("xa_ready")
        turned = sem("turned")
        aT_lo = sem("aT_lo")
        aT_hi = sem("aT_hi")
        prep_mm = sem("prep_mm")
        prep_cp = sem("prep_cp")
        prep_dve = sem("prep_dve")
        qv_ready = sem("qv_ready")
        sc_ready = sem("sc_ready")
        exp_ready = sem("exp_ready")
        fproj = sem("fproj")
        sxv_ready = sem("sxv_ready")
        resid_ready = sem("resid_ready")
        om_ready = sem("om_ready")
        om_turned = sem("om_turned")
        omT_a = sem("omT_a")
        omT_b = sem("omT_b")
        gate_ready = sem("gate_ready")
        fc1_ready = sem("fc1_ready")
        hT_ready = sem("hT_ready")
        fc2_ready = sem("fc2_ready")
        w1_ready = sem("w1_ready")
        gT_ready = sem("gT_ready")
        mlog_ready = sem("mlog_ready")
        y_ready = sem("y_ready")
        wsel_ready = sem("wsel_ready")
        wsel_turned = sem("wsel_turned")
        wselT_ready = sem("wselT_ready")
        base_ready = sem("base_ready")
        fin_ready = sem("fin_ready")
        out_done = sem("out_done")
        dve_step = sem("dve_step")
        act_step = sem("act_step")

        block = ctx.enter_context(nc.Block())

        @block.sync
        def _(sp):
            sp.dma_start(wt_sb[:, :], w_tok).then_inc(wt_in, 16)
            for m in range(STEPS):
                last = PAIRS if m == STEPS - 1 else STEPS * (m + 1)
                sp.dma_start(x_sb[:, STEPS * m:last, :], x[:, STEPS * m:last, :]).then_inc(x_in[m], 16)
            sp.dma_start(wd_sb[:, :, :], wd).then_inc(wd_in, 16)
            sp.wait_ge(fin_ready, 1)
            sp.dma_start(out, fin[:, :, :]).then_inc(out_done, 16)
            sp.wait_ge(out_done, 16)

        @block.gpsimd
        def _(pool):
            pass

        @block.tensor
        def _(pe):
            def mm(o, lhsT, rhs, start=True, stop=True, **k):
                return nc.tensor.matmul(o, lhsT, rhs, start=start, stop=stop, **k)

            pe.wait_ge(c65_in, 16)
            mm(bank[3][0:D, 0:D], c6("a0_q", D), c6("a0_k", D))
            last = None
            for e in range(NE):
                a = W65["bd_q"][0] + e * D
                last = mm(bank[4][0:D, e * D:(e + 1) * D], c65[0:D, a:a + D], c6("bd_k", D))
            mm(bank[5][0:D + 1, 0:D + 1], c6("a1_q", D), c6("a1_k", D))
            mm(bank[5][0:D + 1, D + 1:2 * D + 1], c6("a1_v", D), c6("a1_o", D))
            mm(bank[6][0:D + 1, 0:D], c6("hl_t", D), c6("bd_v", D)).then_inc(prep_mm, 1)
            pe.wait_ge(prep_cp, 2)
            mm(bank[7][0:D + 1, 0:NE * D], c6("hl_t", D), mq[:, :]).then_inc(prep_mm, 1)

            h_ps = bank[0]
            mm(h_ps[:, 0:S * D], c6("ones", 1), c6("tok_b", 1), stop=False, skip_group_check=True)
            pe.wait_ge(wt_in, 16)
            for q in range(PAIRS):
                m, j = divmod(q, STEPS)
                if j == 0 and m < STEPS:
                    pe.wait_ge(x_in[m], 16)
                lo = m - 2 if j == 0 else m - 1
                hi = m
                w0 = 0 if j == 0 else D + 2 * D * j
                if lo < 0:
                    w0 -= lo * D
                    lo = 0
                hi = min(hi, S - 1)
                n = hi - lo + 1
                last = mm(h_ps[:, lo * D:(hi + 1) * D], x_sb[:, q, :], wt_sb[:, w0:w0 + n * D],
                          start=False, stop=(q == PAIRS - 1), skip_group_check=True)
            last.then_inc(tok_done, 1)

            def turn(src, rows, k):
                for s in range(S):
                    o = bank[1][0:rows, s * B:(s + 1) * B] if s < S0 else bank[2][0:rows, (s - S0) * B:(s - S0 + 1) * B]
                    t = nc.tensor.transpose(o, src[:, s, 0:rows], ident)
                    if s in (S0 - 1, S - 1):
                        t.then_inc(turned, 1)

            def attention(rows, w, cols):
                for s in range(S):
                    if s == 0:
                        pass
                    o = bank[3][:, s * cols:(s + 1) * cols] if s < S0 else bank[4][:, (s - S0) * cols:(s - S0 + 1) * cols]
                    t = mm(o, aT[0:rows, s, :], w)
                    if s in (S0 - 1, S - 1):
                        t.then_inc(qv_ready, 1)

            pe.wait_ge(c128_in, 16)
            pe.wait_ge(xa_ready, 1)
            turn(xa, D + 1, 0)
            pe.wait_ge(aT_lo, 1)
            pe.wait_ge(aT_hi, 1)
            pe.wait_ge(prep_cp, 6)
            pe.wait_ge(prep_dve, 2)
            attention(D, t0q[:, :], 2 * D)

            pe.wait_ge(xa_ready, 2)
            turn(xa, D + 1, 1)
            pe.wait_ge(aT_lo, 2)
            pe.wait_ge(aT_hi, 2)
            for s in range(S):
                mm(bank[3 + s][:, 0:2 * D + NE * D], aT[:, s, :], wf[:, :]).then_inc(fproj, 1)
            pe.wait_ge(sxv_ready, S)
            for n in range(NH):
                a = W128["onehot"][0] + n * 128
                last = mm(bank[0][:, n * S * DH:(n + 1) * S * DH], c128[0:NH, a:a + 128],
                          sxv[0:NH, :, n * DH:(n + 1) * DH])
            last.then_inc(resid_ready, 1)
            for s in range(S):
                pe.wait_ge(om_ready, s + 1)
                for c in range(2):
                    i = 2 * s + c
                    t = nc.tensor.transpose(bank[3 + i // 4][:, (i % 4) * B:(i % 4 + 1) * B],
                                            om[:, s, c * 128:(c + 1) * 128], ident)
                    if i in (3, 7, 9):
                        t.then_inc(om_turned, 1)
            for s in range(S):
                for c in range(2):
                    i = 2 * s + c
                    if i == 0:
                        pe.wait_ge(omT_a, 1)
                    if i == 4:
                        pe.wait_ge(omT_b, 1)
                    if i == 8:
                        pe.wait_ge(omT_a, 2)
                    a = W128["gate_w"][0] + c * NE * NH
                    last = mm(bank[1][:, s * NE * NH:(s + 1) * NE * NH], omT[:, i, :], c128[:, a:a + NE * NH],
                              start=(c == 0), stop=(c == 1))
            last.then_inc(gate_ready, 1)
            pe.wait_ge(xa_ready, 3)
            turn(f1, D + 1, 2)
            pe.wait_ge(aT_lo, 3)
            mm(bank[3][0:D, 0:S0 * B], c6("fc1"), aT[:, 0:S0, :]).then_inc(fc1_ready, 1)
            pe.wait_ge(aT_hi, 3)
            mm(bank[4][0:D, 0:(S - S0) * B], c6("fc1"), aT[:, S0:S, :]).then_inc(fc1_ready, 1)
            pe.wait_ge(hT_ready, 2)
            for s in range(S):
                last = mm(bank[5][:, s * D:(s + 1) * D], hT[:, s, :], c6("fc2"))
            last.then_inc(fc2_ready, 1)

            pe.wait_ge(xa_ready, 4)
            turn(xa, D + 1, 3)
            pe.wait_ge(aT_lo, 4)
            pe.wait_ge(aT_hi, 4)
            attention(D + 1, t1q[:, :], 2 * D + 1)

            pe.wait_ge(xa_ready, 5)
            turn(xa, D + 1, 4)
            pe.wait_ge(aT_lo, 5)
            pe.wait_ge(aT_hi, 5)
            w1 = W65["w1"][0]
            for c in range(KC):
                wc = c65[:, w1 + c * 128:w1 + (c + 1) * 128]
                mm(bank[3 + 2 * c][:, 0:S0 * B], wc, aT[:, 0:S0, :]).then_inc(w1_ready, 1)
                mm(bank[4 + 2 * c][:, 0:(S - S0) * B], wc, aT[:, S0:S, :]).then_inc(w1_ready, 1)
            pe.wait_ge(gT_ready, 4)
            wg = W128["wg"][0]
            for s in range(S):
                for c in range(KC):
                    last = mm(bank[0][:, s * E:(s + 1) * E], gT[:, c, s, :], c128[:, wg + c * E:wg + (c + 1) * E],
                              start=(c == 0), stop=(c == KC - 1))
            last.then_inc(mlog_ready, 1)
            pe.wait_ge(wd_in, 16)
            for s in range(S):
                for c in range(KC):
                    last = mm(bank[1 + s][:, :], gT[:, c, s, :], wd_sb[:, c, :], start=(c == 0), stop=(c == KC - 1))
                last.then_inc(y_ready, 1)
                if s == 1:
                    pe.wait_ge(wsel_ready, 1)
                    nc.tensor.transpose(bank[7][0:S * E, 0:B], wsel[:, :, :].rearrange("b s e -> b (s e)"),
                                        ident).then_inc(wsel_turned, 1)
                    mm(bank[6][:, 0:S * D], ident, h[:, :, :], stop=False)
                    pe.wait_ge(wselT_ready, 1)
                    mm(bank[6][:, 0:S * D], wselT[:, :], c1("bd")[0:S * E, :], start=False).then_inc(base_ready, 1)

        @block.scalar
        def _(act):
            steps = [0]

            def link(ins):
                steps[0] += 1
                ins.then_inc(act_step, 1)
                act.wait_ge(act_step, steps[0])

            act.dma_start(c65[:, :], w65).then_inc(c65_in, 16)
            act.dma_start(c128[:, :], w128).then_inc(c128_in, 16)
            nc.scalar.preload_act_table_set("gelu_and_others")
            act.wait_ge(prep_mm, 1)
            nc.scalar.copy(t0q[:, 0:D], bank[3][0:D, 0:D]).then_inc(prep_cp, 1)
            nc.scalar.copy(mq[:, :], bank[4][0:D, 0:NE * D]).then_inc(prep_cp, 1)
            nc.scalar.copy(wf[:, D:2 * D], bank[6][0:D + 1, 0:D]).then_inc(prep_cp, 1)
            nc.scalar.copy(wf[:, 0:D], c6("hl")).then_inc(prep_cp, 1)
            nc.scalar.copy(t0q[:, D:2 * D], c6("a0_v", D)).then_inc(prep_cp, 1)
            act.wait_ge(prep_mm, 2)
            nc.scalar.copy(wf[:, 2 * D:], bank[7][0:D + 1, 0:NE * D]).then_inc(prep_cp, 1)

            act.wait_ge(tok_done, 1)
            nc.scalar.activation(h[:, :, :], bank[0][:, 0:S * D].rearrange("b (s d) -> b s d", d=D),
                                 ACT.Gelu).then_inc(h_ready, 1)
            nc.scalar.preload_act_table_set("natural_log_exp_and_others")

            def inverse_std(k, out_, tmp, var, scale, eps):
                act.wait_ge(var_ready, k)
                link(nc.scalar.activation(tmp, var, ACT.Ln, bias=eps[:, :], scale=scale))
                nc.scalar.activation(out_, tmp, ACT.Exp, scale=-0.5).then_inc(rstd_ready, 1)

            def evacuate_turned(k):
                act.wait_ge(turned, 2 * k - 1)
                nc.scalar.copy(aT[:, 0:S0, :], bank[1][0:D + 1, 0:S0 * B].rearrange("d (s b) -> d s b", b=B)
                               ).then_inc(aT_lo, 1)

            def exponent(k, out_, in_, scale=1.0):
                act.wait_ge(sc_ready, k)
                nc.scalar.activation(out_, in_, ACT.Exp, scale=scale).then_inc(exp_ready, 1)

            inverse_std(1, rstd[:, :], lnv[:, :], ag[:, :, 1], 1.0, c_eps)
            evacuate_turned(1)
            exponent(1, p[:, :, :], sc[:, :, :])
            inverse_std(2, rstd[:, :], lnv[:, :], ag[:, :, 1], 1.0, c_eps)
            evacuate_turned(2)
            for s in range(S):
                act.wait_ge(fproj, s + 1)
                nc.scalar.copy(sxv[:, s, :], bank[3 + s][:, 0:2 * D]).then_inc(sxv_ready, 1)
            exponent(2, fp[:, :, :, :], fs[:, :, :, :], scale=float(DH) ** 0.5)
            act.wait_ge(om_turned, 1)
            nc.scalar.copy(omT[:, 0:4, :], bank[3][:, :].rearrange("p (i b) -> p i b", b=B)).then_inc(omT_a, 1)
            act.wait_ge(om_turned, 3)
            nc.scalar.copy(omT[:, 8:10, :], bank[5][:, 0:2 * B].rearrange("p (i b) -> p i b", b=B)).then_inc(omT_a, 1)
            exponent(3, gs[:, :, :], lg[:, :, :])
            inverse_std(3, rs[:, :], ls[:, :], s2[:, :], 1.0 / DH, c_epsf)
            evacuate_turned(3)
            inverse_std(4, rs[:, :], ls[:, :], s2[:, :], 1.0 / DH, c_epsf)
            exponent(4, fge[:, :, :], fg[:, :, :])
            inverse_std(5, rstd[:, :], lnv[:, :], ag[:, :, 1], 1.0, c_eps)
            evacuate_turned(4)
            exponent(5, p[:, :, :], sc[:, :, :], scale=float(D) ** -0.5)
            inverse_std(6, rstd[:, :], lnv[:, :], ag[:, :, 1], 1.0, c_eps)
            nc.scalar.preload_act_table_set("gelu_and_others")
            evacuate_turned(5)
            for c in range(KC):
                act.wait_ge(w1_ready, 2 * c + 1)
                nc.scalar.activation(gT[:, c, 0:S0, :], bank[3 + 2 * c][:, 0:S0 * B].rearrange("p (s b) -> p s b", b=B),
                                     ACT.Gelu).then_inc(gT_ready, 1)
                act.wait_ge(w1_ready, 2 * c + 2)
                nc.scalar.activation(gT[:, c, S0:S, :],
                                     bank[4 + 2 * c][:, 0:(S - S0) * B].rearrange("p (s b) -> p s b", b=B),
                                     ACT.Gelu).then_inc(gT_ready, 1)
            nc.scalar.preload_act_table_set("natural_log_exp_and_others")
            exponent(6, me[:, :, :], mt[:, :, :])
            act.wait_ge(wsel_turned, 1)
            nc.scalar.copy(wselT[:, :], bank[7][0:S * E, 0:B]).then_inc(wselT_ready, 1)

        @block.vector
        def _(dve):
            V = nc.vector
            steps = [0]

            def link(ins):
                steps[0] += 1
                ins.then_inc(dve_step, 1)
                dve.wait_ge(dve_step, steps[0])

            def over(ap, n, at):
                shape = list(ap.shape)
                return ap.unsqueeze(at).broadcast_to(shape[:at] + [n] + shape[at:])

            link(V.memset(xa[:, :, D:D + 1], 1.0))
            link(V.memset(f1[:, :, D:D + 1], 1.0))
            link(V.memset(hT[D:D + 1, :, :], 1.0))
            link(V.memset(fs[:, :, :, :], -1e30))
            V.memset(c_eps[:, :], EPS)
            link(V.memset(c_epsf[:, :], EPS_FFN))

            dve.wait_ge(prep_mm, 1)
            V.tensor_copy(t1q[:, 0:D + 1], bank[5][0:D + 1, 0:D + 1]).then_inc(prep_dve, 1)
            V.tensor_tensor(t1q[:, D + 1:], bank[5][0:D + 1, D + 1:2 * D + 1], c6("bo"), ALU.add).then_inc(prep_dve, 1)

            def normalise(k_h, k_var, k_rstd):
                for s in range(S):
                    last = V.bn_stats(st[:, s, :], h[:, s, :])
                link(last)
                for s in range(S):
                    last = V.bn_aggr(ag[:, s, :], st[:, s, :])
                last.then_inc(var_ready, 1)
                dve.wait_ge(var_ready, k_var)
                link(V.tensor_tensor(xc[:, :, :], h[:, :, :], over(ag[:, :, 0], D, 2), ALU.subtract))
                dve.wait_ge(rstd_ready, k_rstd)
                V.tensor_tensor(xa[:, :, 0:D], xc[:, :, :], over(rstd[:, :], D, 2), ALU.mult).then_inc(xa_ready, 1)

            def evacuate_turned(k):
                dve.wait_ge(turned, 2 * k)
                V.tensor_copy(aT[:, S0:S, :], bank[2][0:D + 1, 0:(S - S0) * B].rearrange("d (s b) -> d s b", b=B)
                              ).then_inc(aT_hi, 1)

            def attention(k, width, scale):
                cols = width + D
                for i, (a, b) in enumerate(((0, S0), (S0, S))):
                    dve.wait_ge(qv_ready, 2 * (k - 1) + i + 1)
                    n = b - a
                    qb = bank[3 + i][:, 0:n * cols].rearrange("b (s c) -> b s c", c=cols)[:, :, 0:width]
                    pr = prod[:, a * S * width:b * S * width].rearrange("b (s t d) -> b s t d", t=S, d=width)
                    link(V.tensor_tensor(pr, over(qb, S, 2), over(xa[:, :, 0:width], n, 1), ALU.mult))
                    link(V.tensor_reduce(sc[:, a:b, :], pr, X, ALU.add))
                link(V.tensor_reduce(mx[:, :], sc[:, :, :], X, ALU.max))
                V.tensor_tensor(sc[:, :, :], sc[:, :, :], over(mx[:, :], S, 2), ALU.subtract).then_inc(sc_ready, 1)
                dve.wait_ge(exp_ready, {1: 1, 2: 5}[k])
                link(V.tensor_reduce(sm[:, :], p[:, :, :], X, ALU.add))
                link(V.reciprocal(sm[:, :], sm[:, :]))
                link(V.scalar_tensor_tensor(p[:, :, :], p[:, :, :], scale, over(sm[:, :], S, 2), ALU.mult, ALU.mult))
                pr = prod[:, 0:S * S * D].rearrange("b (s t d) -> b s t d", t=S, d=D)
                for i, (a, b) in enumerate(((0, S0), (S0, S))):
                    n = b - a
                    vb = bank[3 + i][:, 0:n * cols].rearrange("b (s c) -> b s c", c=cols)[:, :, width:cols]
                    last = V.tensor_tensor(pr[:, :, a:b, :], over(vb, S, 1), over(p[:, :, a:b], D, 3), ALU.mult)
                link(last)
                link(V.tensor_reduce(att[:, :, :], pr.rearrange("b s t d -> b s d t"), X, ALU.add))
                link(V.tensor_tensor(h[:, :, :], h[:, :, :], att[:, :, :], ALU.add))

            def inner_norm(k_var, g, b, out_):
                link(V.tensor_reduce(s1[:, :], y[:, :, :], X, ALU.add))
                link(V.scalar_tensor_tensor(yc[:, :, :], over(s1[:, :], DH, 2), -1.0 / DH, y[:, :, :], ALU.mult, ALU.add))
                link(V.tensor_tensor(sq[:, :, :], yc[:, :, :], yc[:, :, :], ALU.mult))
                V.tensor_reduce(s2[:, :], sq[:, :, :], X, ALU.add).then_inc(var_ready, 1)
                dve.wait_ge(rstd_ready, k_var)
                link(V.tensor_tensor(yc[:, :, :], yc[:, :, :], over(rs[:, :], DH, 2), ALU.mult))
                ys = yc[:, :, :].rearrange("b (s n) d -> b s (n d)", n=NH)
                link(V.tensor_tensor(ys, ys, over(g, S, 1), ALU.mult))
                return V.tensor_tensor(out_, ys, over(b, S, 1), ALU.add)

            dve.wait_ge(h_ready, 1)
            normalise(1, 1, 1)
            evacuate_turned(1)
            attention(1, D, float(D) ** -0.5)

            normalise(2, 2, 2)
            evacuate_turned(2)
            for s in range(S):
                dve.wait_ge(sxv_ready, s + 1)
                n = s + 1
                q4 = bank[3 + s][:, 2 * D:2 * D + NE * D].rearrange("b (e c) -> b e c", e=NE)
                pr = fprod[:, 0:n * NE * D]
                link(V.tensor_tensor(pr.rearrange("b (e t c) -> b e t c", e=NE, c=D), over(q4, n, 2),
                                     over(sxv[:, 0:n, 0:D], NE, 1), ALU.mult))
                for e in range(NE):
                    last = V.tensor_reduce(fs[:, s, 0:n, e * NH:(e + 1) * NH],
                                           pr[:, e * n * D:(e + 1) * n * D].rearrange("b (t h d) -> b t h d", h=NH, d=DH),
                                           X, ALU.add)
                link(last)
            link(V.tensor_scalar(notpad[:, :, :], sxv[:, :, 0:D], 0.0, None, ALU.not_equal))
            link(V.tensor_reduce(fm[:, :, :], fs[:, :, :, :].rearrange("b s t c -> b s c t"), X, ALU.max))
            V.tensor_tensor(fs[:, :, :, :], fs[:, :, :, :], over(fm[:, :, :], S, 2), ALU.subtract).then_inc(sc_ready, 1)
            dve.wait_ge(exp_ready, 2)
            link(V.tensor_reduce(fr[:, :, :], fp[:, :, :, :].rearrange("b s t c -> b s c t"), X, ALU.add))
            link(V.reciprocal(fr[:, :, :], fr[:, :, :]))
            link(V.tensor_tensor(fp[:, :, :, :], fp[:, :, :, :], over(fr[:, :, :], S, 2), ALU.mult))
            for s in range(S):
                n = s + 1
                pr = fprod[:, 0:n * NE * D].rearrange("b (t c) -> b t c", t=n)
                for t in range(n):
                    v4 = sxv[:, t, D:2 * D].rearrange("b (h d) -> b h d", h=NH)
                    p4 = fp[:, s, t, :].rearrange("b (e h) -> b e h", h=NH)
                    last = V.tensor_tensor(pr[:, t, :].rearrange("b (e h d) -> b e h d", e=NE, h=NH),
                                           over(v4, NE, 1), over(p4, DH, 3), ALU.mult)
                link(last)
                link(V.tensor_reduce(om[:, s, :], pr.rearrange("b t c -> b c t"), X, ALU.add))
                o4 = om[:, s, :].rearrange("b (e c) -> b e c", e=NE)
                V.tensor_tensor(o4, o4, over(notpad[:, s, :], NE, 1), ALU.mult).then_inc(om_ready, 1)
            dve.wait_ge(om_turned, 2)
            V.tensor_copy(omT[:, 4:8, :], bank[4][:, :].rearrange("p (i b) -> p i b", b=B)).then_inc(omT_b, 1)
            dve.wait_ge(gate_ready, 1)
            link(V.tensor_tensor(lg[:, :, :], bank[1][:, 0:S * NE * NH].rearrange("b (s c) -> b s c", s=S),
                                 over(c1("gate_b"), S, 1), ALU.add))
            lgv = lg[:, :, :].rearrange("b s (e h) -> b s h e", h=NH)
            link(V.tensor_reduce(gm[:, :, :], lgv, X, ALU.max))
            V.tensor_tensor(lg[:, :, :].rearrange("b s (e h) -> b s e h", h=NH),
                            lg[:, :, :].rearrange("b s (e h) -> b s e h", h=NH), over(gm[:, :, :], NE, 2),
                            ALU.subtract).then_inc(sc_ready, 1)
            dve.wait_ge(exp_ready, 3)
            link(V.tensor_reduce(gr[:, :, :], gs[:, :, :].rearrange("b s (e h) -> b s h e", h=NH), X, ALU.add))
            link(V.reciprocal(gr[:, :, :], gr[:, :, :]))
            g4 = gs[:, :, :].rearrange("b s (e h) -> b s e h", h=NH)
            link(V.tensor_tensor(g4, g4, over(gr[:, :, :], NE, 2), ALU.mult))
            o3 = om[:, :, :].rearrange("b s (c d) -> b (s c) d", d=DH)
            pr = fprod[:, 0:S * NE * D]
            link(V.tensor_tensor(pr.rearrange("b (c d) -> b c d", d=DH), o3,
                                 over(gs[:, :, :].rearrange("b s c -> b (s c)"), DH, 2), ALU.mult))
            yv = y[:, :, :].rearrange("b (s n) d -> b s (n d)", n=NH)
            link(V.tensor_reduce(yv, pr.rearrange("b (s e c) -> b s c e", s=S, e=NE), X, ALU.add))
            dve.wait_ge(resid_ready, 1)
            y4 = y[:, :, :].rearrange("b (s n) d -> b s n d", n=NH)
            link(V.tensor_tensor(y4, y4, bank[0][:, 0:S * D].rearrange("b (n s d) -> b s n d", n=NH, s=S), ALU.add))
            inner_norm(3, c1("ln_g"), c1("ln_b"), f1[:, :, 0:D]).then_inc(xa_ready, 1)
            dve.wait_ge(xa_ready, 3)
            evacuate_turned(3)
            V.tensor_scalar(m1[:, :, :], f1[:, :, 0:D], 0.0, None, ALU.not_equal)
            dve.wait_ge(aT_lo, 3)
            dve.wait_ge(aT_hi, 3)
            link(V.tensor_scalar(m1T[:, :, :], aT[0:D, :, :], 0.0, None, ALU.not_equal))
            dve.wait_ge(fc1_ready, 1)
            V.scalar_tensor_tensor(hT[0:D, 0:S0, :], bank[3][0:D, 0:S0 * B].rearrange("d (s b) -> d s b", b=B), 0.0,
                                   m1T[:, 0:S0, :], ALU.max, ALU.mult).then_inc(hT_ready, 1)
            dve.wait_ge(fc1_ready, 2)
            V.scalar_tensor_tensor(hT[0:D, S0:S, :], bank[4][0:D, 0:(S - S0) * B].rearrange("d (s b) -> d s b", b=B), 0.0,
                                   m1T[:, S0:S, :], ALU.max, ALU.mult).then_inc(hT_ready, 1)
            dve.wait_ge(fc2_ready, 1)
            link(V.tensor_tensor(yv, bank[5][:, 0:S * D].rearrange("b (s d) -> b s d", s=S), m1[:, :, :], ALU.mult))
            link(V.tensor_tensor(yv, yv, f1[:, :, 0:D], ALU.add))
            link(inner_norm(4, c1("fn_g"), c1("fn_b"), fo[:, :, :]))
            pr = fprod[:, 0:S * NH * D].rearrange("b (s n c) -> b s n c", s=S, n=NH)
            link(V.tensor_tensor(pr, over(fo[:, :, :], NH, 2),
                                 over(c1("fgate").rearrange("b (n c) -> b n c", n=NH), S, 1), ALU.mult))
            link(V.tensor_reduce(fg[:, :, :], pr, X, ALU.add))
            link(V.tensor_reduce(fgm[:, :], fg[:, :, :], X, ALU.max))
            V.tensor_tensor(fg[:, :, :], fg[:, :, :], over(fgm[:, :], NH, 2), ALU.subtract).then_inc(sc_ready, 1)
            dve.wait_ge(exp_ready, 4)
            link(V.tensor_reduce(fgr[:, :], fge[:, :, :], X, ALU.add))
            link(V.reciprocal(fgr[:, :], fgr[:, :]))
            link(V.tensor_tensor(fge[:, :, :], fge[:, :, :], over(fgr[:, :], NH, 2), ALU.mult))
            fo3 = fo[:, :, :].rearrange("b s (n d) -> b (s n) d", n=NH)
            link(V.tensor_tensor(yc[:, :, :], fo3, over(fge[:, :, :].rearrange("b s n -> b (s n)"), DH, 2), ALU.mult))
            link(V.tensor_tensor(h[:, :, :], h[:, :, :], yc[:, :, :].rearrange("b (s n) d -> b s (n d)", n=NH), ALU.add))

            normalise(3, 5, 5)
            evacuate_turned(4)
            attention(2, D + 1, 1.0)

            normalise(4, 6, 6)
            evacuate_turned(5)
            dve.wait_ge(mlog_ready, 1)
            link(V.tensor_tensor(ml[:, :, :], bank[0][:, 0:S * E].rearrange("b (s e) -> b s e", s=S),
                                 over(c1("bg"), S, 1), ALU.add))
            link(V.tensor_reduce(mm_[:, :], ml[:, :, :], X, ALU.max))
            V.tensor_tensor(mt[:, :, :], ml[:, :, :], over(mm_[:, :], E, 2), ALU.subtract).then_inc(sc_ready, 1)
            dve.wait_ge(exp_ready, 6)
            link(V.tensor_reduce(mr[:, :], me[:, :, :], X, ALU.add))
            link(V.reciprocal(mr[:, :], mr[:, :]))
            link(V.tensor_tensor(mp[:, :, :], me[:, :, :], over(mr[:, :], E, 2), ALU.mult))
            link(V.tensor_reduce(mm_[:, :], mp[:, :, :], X, ALU.max))
            link(V.tensor_tensor(mt[:, :, :], mp[:, :, :], over(mm_[:, :], E, 2), ALU.is_equal))
            link(V.tensor_tensor(mt[:, :, :], mt[:, :, :], over(c1("first"), S, 1), ALU.mult))
            link(V.tensor_reduce(mm_[:, :], mt[:, :, :], X, ALU.max))
            link(V.tensor_tensor(mt[:, :, :], mt[:, :, :], over(mm_[:, :], E, 2), ALU.is_equal))
            V.tensor_tensor(wsel[:, :, :], mt[:, :, :], mp[:, :, :], ALU.mult).then_inc(wsel_ready, 1)
            dve.wait_ge(wsel_ready, 1)
            for s in range(S):
                dve.wait_ge(y_ready, s + 1)
                pr = yprod[:, s % 2, :].rearrange("b (e c) -> b e c", e=E)
                link(V.tensor_tensor(pr, bank[1 + s][:, :].rearrange("b (e c) -> b e c", e=E),
                                     over(wsel[:, s, :], D, 2), ALU.mult))
                link(V.tensor_reduce(ysum[:, s, :], pr.rearrange("b e c -> b c e"), X, ALU.add))
            dve.wait_ge(base_ready, 1)
            V.tensor_tensor(fin[:, :, :], bank[6][:, 0:S * D].rearrange("b (s d) -> b s d", s=S), ysum[:, :, :],
                            ALU.add).then_inc(fin_ready, 1)


def kernel(**inputs):
    import numpy as np
    import concourse.bacc as _bacc
    from concourse import mybir as _mybir
    from concourse.bass_utils import run_bass_kernel_spmd as _run

    i = {k: np.asarray(v) for k, v in inputs.items()}
    f = np.float32
    x = i["x"][:, 0, :PH, :2 * PAIRS].reshape(B, PH, PAIRS, 2).transpose(3, 1, 2, 0).reshape(128, PAIRS, B)
    wt = i["L0_tok_weight"].reshape(PH, PW, D)
    tok = np.zeros((2, PH, D + STEPS * 2 * D), f)
    tok[0, :, 0:D] = wt[:, PW - 1]
    for j in range(STEPS):
        for c in range(2):
            a = D + 2 * D * j
            tok[c, :, a:a + D] = wt[:, SW + 2 * j + c]
            tok[c, :, a + D:a + 2 * D] = wt[:, 2 * j + c]
    tok = tok.reshape(128, -1)

    w128 = np.zeros((128, N128), f)
    w65 = np.zeros((65, N65), f)

    def put(pack, table, name, block, at=0):
        a = table[name][0] + at
        pack[:block.shape[0], a:a + block.shape[1]] = block

    put(w128, W128, "ident", np.eye(128, dtype=f))
    put(w128, W128, "wg", i["L1_ffn_Wg"].reshape(KC, 128, E).transpose(1, 0, 2).reshape(128, -1))
    gw = np.zeros((NE, NH, DH, NE, NH), f)
    gate_w = i["L0_ffn_gate_w"].reshape(NH, NE, NE, DH)
    for n in range(NH):
        gw[:, n, :, :, n] = gate_w[n].transpose(1, 2, 0)
    put(w128, W128, "gate_w", gw.reshape(2, 128, NE * NH).transpose(1, 0, 2).reshape(128, -1))
    put(w128, W128, "onehot", np.repeat(np.eye(NH, dtype=f), 128, axis=1))
    put(w128, W128, "gate_b", np.broadcast_to(i["L0_ffn_gate_b"].T.reshape(1, -1), (128, NE * NH)))
    for n, src in (("ln_g", "ln_g"), ("ln_b", "ln_b"), ("fn_g", "fnorm_g"), ("fn_b", "fnorm_b")):
        put(w128, W128, n, np.broadcast_to(np.tile(i["L0_ffn_" + src], NH)[None], (128, D)))
    put(w128, W128, "fgate", np.broadcast_to(i["L0_ffn_fgate_w"].reshape(1, -1), (128, NH * D)))
    put(w128, W128, "bg", np.broadcast_to(i["L1_ffn_bg"][None], (128, E)))
    put(w128, W128, "first", np.broadcast_to(np.arange(E, 0, -1, dtype=f)[None], (128, E)))
    bd = np.zeros((S, E, S, D), f)
    for s in range(S):
        bd[s, :, s, :] = i["L1_ffn_bd"]
    put(w128, W128, "bd", bd.reshape(S * E, S * D))

    def heads(w):
        m = np.zeros((NH, DH, NH, DH), f)
        for n in range(NH):
            m[n, :, n, :] = w[n]
        return m.reshape(D, D)

    def same(w):
        return heads(np.broadcast_to(w, (NH, DH, DH)))

    def col(a, b):
        return np.concatenate([a, b.reshape(-1, 1)], axis=1)

    def row(a, b):
        return np.concatenate([a, b.reshape(1, -1)], axis=0)

    put(w65, W65, "a0_q", i["L0_attn_Wq"])
    put(w65, W65, "a0_k", i["L0_attn_Wk"])
    put(w65, W65, "a0_v", i["L0_attn_Wv"].T)
    hl = i["L0_ffn_hl_w"].reshape(D, D)
    put(w65, W65, "hl_t", col(hl, i["L0_ffn_hl_b"].reshape(-1)))
    put(w65, W65, "hl", row(hl.T, i["L0_ffn_hl_b"].reshape(-1)))
    put(w65, W65, "bd_v", heads(i["L0_ffn_wv"].transpose(0, 2, 1)))
    for e in range(NE):
        put(w65, W65, "bd_q", heads(i["L0_ffn_wq"][:, e]), e * D)
    put(w65, W65, "bd_k", heads(i["L0_ffn_wk"]))
    put(w65, W65, "fc1", row(same(i["L0_ffn_fc1_w"].T), np.tile(i["L0_ffn_fc1_b"], NH)))
    put(w65, W65, "fc2", row(same(i["L0_ffn_fc2_w"].T), np.tile(i["L0_ffn_fc2_b"], NH)))
    put(w65, W65, "a1_q", col(i["L1_attn_Wq"], i["L1_attn_bq"]))
    put(w65, W65, "a1_k", col(i["L1_attn_Wk"], i["L1_attn_bk"]))
    put(w65, W65, "a1_v", col(i["L1_attn_Wv"], i["L1_attn_bv"]))
    put(w65, W65, "a1_o", i["L1_attn_Wo"].T)
    put(w65, W65, "w1", row(i["L1_ffn_W1"], i["L1_ffn_b1"]))
    put(w65, W65, "bo", row(np.zeros((D, D), f), i["L1_attn_bo"]))
    put(w65, W65, "tok_b", np.tile(i["L0_tok_bias"], S)[None])
    put(w65, W65, "ones", np.ones((1, 128), f))
    wd = i["L1_ffn_Wd"].transpose(1, 0, 2).reshape(KC, 128, E * D).transpose(1, 0, 2)

    nc = _bacc.Bacc("TRN2", target_bir_lowering=False, num_devices=1)
    arrays, args = {}, []
    for name, a in (("x", x), ("w_tok", tok), ("w128", w128), ("w65", w65), ("wd", wd)):
        arrays[f"in_{name}"] = np.ascontiguousarray(a)
        args.append(nc.dram_tensor(f"in_{name}", a.shape, _mybir.dt.from_np(a.dtype), kind="ExternalInput").ap())
    args.append(nc.dram_tensor("out_0", (B, S, D), _mybir.dt.from_np(np.dtype(f)), kind="ExternalOutput").ap())
    vit_tower_kernel(nc, *args)
    r = _run(nc, [arrays], core_ids=[0])
    return r.results[0]["out_0"]
```

```python
import concourse.bass as bass
from concourse import mybir
from contextlib import ExitStack

B, S, D = 128, 5, 64
PH, PW, SW = 64, 25, 12
PAIRS = (SW * (S - 1) + PW + 1) // 2
STEPS = SW // 2
NH, DH, NE = 4, 16, 4
NC = NE * NH
HID, E = 256, 8
KC = HID // 128
EPS, EPS_FFN = 1e-5, 1e-8
S0 = 3
S1 = S - S0
XCHUNKS = [(0, 2), (2, 6), (6, 12), (12, 18), (18, 24), (24, 30), (30, PAIRS)]
WSPLIT = D + 2 * 2 * D


def table(*entries):
    at, found = 0, {}
    for name, count in entries:
        found[name] = (at, count)
        at += count
    return found, at


TOKB, N_TOKB = table(("tok_b", S * D), ("ones", 128))
WA, N_WA = table(("q", D), ("k", D), ("v", D), ("centre", D))
WB, N_WB = table(("hl_t", D + 1), ("hl", D), ("bd_v", D), ("bd_vt", D), ("bd_g", NE * NC), ("bd_q", NE * D),
                 ("bd_k", D), ("fc1", D), ("fc2", D), ("ln_g", 1), ("ln_b", 1), ("fn_g", 1), ("fn_b", 1),
                 ("fg_block", NH * NH), ("fg_t", NH))
WC, N_WC = table(("q", D), ("k", D), ("bk", 1), ("bq", 1), ("v", D), ("bv", 1), ("o_t", D), ("bo", D),
                 ("ones", 128), ("w1", HID))
ROWS, N_ROWS = table(("wg", KC * E), ("gate_b", NC), ("bg", E), ("first", E), ("ln_g", D), ("ln_b", D),
                     ("fn_g", D), ("fn_b", D))


def vit_tower_kernel(nc: bass.Bass, x: bass.AP, w_tok: bass.AP, tokb: bass.AP, ident_in: bass.AP, wa: bass.AP,
                     wb: bass.AP, wc: bass.AP, rows: bass.AP, onehot: bass.AP, bd: bass.AP, gate_rows: bass.AP,
                     wd: bass.AP, out: bass.AP):
    fp32, bf16, i32 = mybir.dt.float32, mybir.dt.bfloat16, mybir.dt.int32
    ALU = mybir.AluOpType
    ACT = mybir.ActivationFunctionType
    X = mybir.AxisListType.X

    ctx = ExitStack()
    with ctx:
        def sb(name, shape, dt=fp32):
            return ctx.enter_context(nc.sbuf_tensor(name, shape, dt))

        def sem(name):
            return ctx.enter_context(nc.semaphore(name))

        x_sb = sb("x_sb", [128, PAIRS, B])
        wt_sb = sb("wt_sb", [128, D + STEPS * 2 * D])
        tokb_sb = sb("tokb_sb", [1, N_TOKB])
        ident = sb("ident", [128, 128])
        wa_sb = sb("wa_sb", [D, N_WA])
        wb_sb = sb("wb_sb", [D + 1, N_WB])
        wc_sb = sb("wc_sb", [D + 1, N_WC])
        rows_sb = sb("rows_sb", [128, N_ROWS])
        onehot_sb = sb("onehot_sb", [NH, NH, 128])
        bd_sb = sb("bd_sb", [S * E, S * D])
        gate_rows_sb = sb("gate_rows_sb", [128, NE, NE * D])
        wd_sb = sb("wd_sb", [128, KC, E * D])
        a0_t1 = sb("a0_t1", [D, D])
        a0_u = sb("a0_u", [D, D])
        a0_w = sb("a0_w", [D, 2 * D])
        f_r = sb("f_r", [D, D + NE * NC + NE * D])
        wf = sb("wf", [D + 1, 2 * D + NE * NC + NE * D])
        a1_t1 = sb("a1_t1", [D, D])
        a1_u = sb("a1_u", [D, D])
        a1_y = sb("a1_y", [D, D + 2])
        a1_w = sb("a1_w", [D, 2 * D + 2])
        a1_c = sb("a1_c", [B, 1 + D])
        fgw = sb("fgw", [D, NH * NH])
        fgc = sb("fgc", [B, NH])
        idle = sb("idle", [128, 512], bf16)
        h = sb("h", [B, S, D])
        hb = sb("hb", [B, S, D])
        st = sb("st", [B, S, 6])
        ag = sb("ag", [B, S, 2])
        lnv = sb("lnv", [B, S])
        rstd = sb("rstd", [B, S])
        rr = sb("rr", [B, S, S])
        ab = sb("ab", [B, S])
        ab2 = sb("ab2", [B, S])
        abst = sb("abst", [B, S, S])
        xc = sb("xc", [B, S, D])
        xa = sb("xa", [B, S, D])
        aT = sb("aT", [D + 1, S, B])
        q_hi = sb("q_hi", [B, S1, D])
        v_sb = sb("v_sb", [B, S, D])
        ab_sb = sb("ab_sb", [B, S, 2])
        prod = sb("prod", [B, S, S, D])
        pvp = sb("pvp", [B, S, S, D])
        sc = sb("sc", [B, S, S])
        mx = sb("mx", [B, S])
        p = sb("p", [B, S, S])
        sm = sb("sm", [B, S])
        att = sb("att", [B, S, D])
        FW = 2 * D + NE * NC
        sxv = sb("sxv", [B, S, FW])
        fq_hi = sb("fq_hi", [B, S1, NE * D])
        fprod = [sb(f"fprod{s}", [B, s + 1, NE * D]) for s in range(S)]
        fs = sb("fs", [B, S, S, NC])
        fm = sb("fm", [B, S, NC])
        fp = sb("fp", [B, S, S, NC])
        fr = sb("fr", [B, S, NC])
        iszero = sb("iszero", [B, S, D])
        pads = sb("pads", [B, 1])
        ones_col = sb("ones_col", [B, 1])
        pads_i = sb("pads_i", [1, 1], i32)
        gprod = [sb(f"gprod{s}", [B, s + 1, NE, NC]) for s in range(S)]
        lg = sb("lg", [B, S, NC])
        lb = sb("lb", [B, S, NC])
        gm = sb("gm", [B, S, NH])
        gs = sb("gs", [B, S, NC])
        gr = sb("gr", [B, S, NH])
        pcp = sb("pcp", [B, S, S, NC])
        pc = sb("pc", [B, S, S, NH])
        mixp = sb("mixp", [B, S, S + 1, D])
        fix_prod = sb("fix_prod", [B, S, NE * D])
        fix_om = sb("fix_om", [B, S, NE * D])
        fix_g = sb("fix_g", [B, S, D])
        fix_np = sb("fix_np", [B, S, D])
        y = sb("y", [B, S * NH, DH])
        yc = sb("yc", [B, S * NH, DH])
        xh = sb("xh", [B, S * NH, DH])
        sq = sb("sq", [B, S * NH, DH])
        s1 = sb("s1", [B, S * NH])
        s2 = sb("s2", [B, S * NH])
        ls = sb("ls", [B, S * NH])
        rs = sb("rs", [B, S * NH])
        f1 = sb("f1", [B, S, D])
        f1g = sb("f1g", [B, S, D])
        m1 = sb("m1", [B, S, D])
        m1T = sb("m1T", [D, S, B])
        hT = sb("hT", [D + 1, S, B])
        fo = sb("fo", [B, S, D])
        fgp = sb("fgp", [B, S, NH, NH])
        fg = sb("fg", [B, S, NH])
        fgm = sb("fgm", [B, S])
        fge = sb("fge", [B, S, NH])
        fgr = sb("fgr", [B, S])
        gT = sb("gT", [128, KC, S, B])
        ml = sb("ml", [B, S, E])
        mlm = sb("mlm", [B, S])
        me = sb("me", [B, S, E])
        mr = sb("mr", [B, S])
        mp = sb("mp", [B, S, E])
        mt = sb("mt", [B, S, E])
        wsel = sb("wsel", [B, S, E])
        wselT = sb("wselT", [S * E, B])
        yprod = sb("yprod", [B, S, E, D])
        ysum = sb("ysum", [B, S, D])
        fin = sb("fin", [B, S, D])
        c_eps = sb("c_eps", [128, 1])
        c_epsf = sb("c_epsf", [128, 1])

        bank = [ctx.enter_context(nc.psum_tensor(f"bank{i}", [128, 512], fp32)) for i in range(8)]

        def part(tile, tab, name, n=None):
            a, c = tab[name]
            return tile[0:n, a:a + c] if n else tile[:, a:a + c]

        wt_in = [sem("wt_in0"), sem("wt_in1")]
        x_in = [sem(f"x_in{m}") for m in range(len(XCHUNKS))]
        tokb_in = sem("tokb_in")
        ident_in_s = sem("ident_in_s")
        wa_in = sem("wa_in")
        wb_in = sem("wb_in")
        wc_in = sem("wc_in")
        rows_in = sem("rows_in")
        onehot_in = sem("onehot_in")
        bd_in = sem("bd_in")
        gate_rows_in = sem("gate_rows_in")
        wd_in = sem("wd_in")
        idle_ready = sem("idle_ready")
        consts_ready = sem("consts_ready")
        tok_done = sem("tok_done")
        h_ready = sem("h_ready")
        var_ready = sem("var_ready")
        rstd_ready = sem("rstd_ready")
        xa_lo = sem("xa_lo")
        xa_hi = sem("xa_hi")
        turned_lo = sem("turned_lo")
        turned_hi = sem("turned_hi")
        aT_lo = sem("aT_lo")
        aT_hi = sem("aT_hi")
        prep_mm = sem("prep_mm")
        prep_cp = sem("prep_cp")
        q_hi_mm = sem("q_hi_mm")
        q_lo_mm = sem("q_lo_mm")
        v_mm = sem("v_mm")
        q_hi_ready = sem("q_hi_ready")
        v_ready = sem("v_ready")
        v_ab = sem("v_ab")
        sprod_hi = sem("sprod_hi")
        hb_ready = sem("hb_ready")
        p_ready = sem("p_ready")
        pvp_hi = sem("pvp_hi")
        sc_ready = sem("sc_ready")
        exp_ready = sem("exp_ready")
        sxv_mm = sem("sxv_mm")
        fq_mm = sem("fq_mm")
        sxv_act = sem("sxv_act")
        sxv_dve = sem("sxv_dve")
        fq_ready = sem("fq_ready")
        fprod_ready = sem("fprod_ready")
        pads_ready = sem("pads_ready")
        pads_mm = sem("pads_mm")
        resid_mm = sem("resid_mm")
        resid_ready = sem("resid_ready")
        fp_ready = sem("fp_ready")
        gprod_ready = sem("gprod_ready")
        pc_ready = sem("pc_ready")
        mixp_ready = sem("mixp_ready")
        yc_ready = sem("yc_ready")
        fc1_ready = sem("fc1_ready")
        hT_ready = sem("hT_ready")
        fc2_ready = sem("fc2_ready")
        fgl_mm = sem("fgl_mm")
        w1_ready = sem("w1_ready")
        gT_ready = sem("gT_ready")
        mlog_ready = sem("mlog_ready")
        y_ready = sem("y_ready")
        wsel_ready = sem("wsel_ready")
        wsel_turned = sem("wsel_turned")
        wselT_ready = sem("wselT_ready")
        base_ready = sem("base_ready")
        fin_ready = sem("fin_ready")
        out_done = sem("out_done")
        dve_step = sem("dve_step")
        act_step = sem("act_step")
        pool_step = sem("pool_step")
        fix_step = sem("fix_step")

        block = ctx.enter_context(nc.Block())

        def over(ap, n, at):
            shape = list(ap.shape)
            return ap.unsqueeze(at).broadcast_to(shape[:at] + [n] + shape[at:])

        LO, HI = slice(0, S0), slice(S0, S)

        def gate_products(engine, s):
            n = s + 1
            pe4 = fp[:, s, 0:n, :].rearrange("b t (e n) -> b (t e) n", n=NH)
            g4 = sxv[:, 0:n, 2 * D:FW].rearrange("b t (e f n) -> b t e f n", e=NE, n=NH)
            o = gprod[s][:, :, :, :].rearrange("b t e (f n) -> b (t e) f n", n=NH)
            last = None
            for t in range(n):
                last = engine.tensor_tensor(o[:, t * NE:(t + 1) * NE, :, :], g4[:, t, :, :, :],
                                            over(pe4[:, t * NE:(t + 1) * NE, :], NE, 2), ALU.mult)
            return last

        def mixed_products(engine, t):
            return engine.tensor_tensor(mixp[:, t:S, 1 + t, :].rearrange("b s (n d) -> b s n d", n=NH),
                                        over(sxv[:, t, D:2 * D].rearrange("b (n d) -> b n d", n=NH), S - t, 1),
                                        over(pc[:, t:S, t, :], DH, 3), ALU.mult)

        @block.sync
        def _(sp):
            def load_x(m):
                a, b = XCHUNKS[m]
                sp.dma_start(x_sb[:, a:b, :], x[:, a:b, :]).then_inc(x_in[m], 16)

            sp.dma_start(wt_sb[:, 0:WSPLIT], w_tok[:, 0:WSPLIT]).then_inc(wt_in[0], 16)
            load_x(0)
            sp.dma_start(wt_sb[:, WSPLIT:], w_tok[:, WSPLIT:]).then_inc(wt_in[1], 16)
            load_x(1)
            load_x(2)
            sp.dma_start(wa_sb[:, :], wa).then_inc(wa_in, 16)
            for m in range(3, len(XCHUNKS)):
                load_x(m)
            sp.dma_start(ident[:, :], ident_in).then_inc(ident_in_s, 16)
            sp.dma_start(tokb_sb[:, :], tokb).then_inc(tokb_in, 16)
            sp.dma_start(wb_sb[:, :], wb).then_inc(wb_in, 16)
            sp.dma_start(wc_sb[:, :], wc).then_inc(wc_in, 16)
            sp.dma_start(rows_sb[:, :], rows).then_inc(rows_in, 16)
            sp.dma_start(onehot_sb[:, :, :], onehot).then_inc(onehot_in, 16)
            sp.dma_start(gate_rows_sb[:, :, :], gate_rows).then_inc(gate_rows_in, 16)
            sp.dma_start(bd_sb[:, :], bd).then_inc(bd_in, 16)
            sp.dma_start(wd_sb[:, :, :], wd).then_inc(wd_in, 16)
            sp.wait_ge(fin_ready, 1)
            sp.dma_start(out, fin[:, :, :]).then_inc(out_done, 16)
            sp.wait_ge(out_done, 16)

        @block.gpsimd
        def _(pool):
            G = nc.gpsimd
            MUL = ALU.mult

            def attention(k, src):
                pool.wait_ge(h_ready, 2 * k - 1)
                pool.wait_ge(q_hi_ready, k)
                for s in range(S1):
                    last = G.tensor_tensor(prod[:, S0 + s, :, :], over(q_hi[:, s, :], S, 1), src[:, :, :], MUL)
                last.then_inc(sprod_hi, 1)
                if k == 2:
                    G.tensor_tensor(hb[:, :, :], h[:, :, :], over(a1_c[:, 1:1 + D], S, 1), ALU.add).then_inc(hb_ready, 1)
                pool.wait_ge(v_ready, k)
                pool.wait_ge(p_ready, k)
                for s in range(S0, S):
                    last = G.tensor_tensor(pvp[:, s, :, :], v_sb[:, :, :], over(p[:, s, :], D, 2), MUL)
                last.then_inc(pvp_hi, 1)

            attention(1, h)

            pool.wait_ge(sxv_act, 2)
            pool.wait_ge(sxv_dve, 1)
            for i, s in enumerate((4, 3)):
                n = s + 1
                pool.wait_ge(fq_ready, i + 1)
                G.tensor_tensor(fprod[s][:, :, :].rearrange("b t (e c) -> b t e c", e=NE),
                                over(fq_hi[:, s - S0, :].rearrange("b (e c) -> b e c", e=NE), n, 1),
                                over(sxv[:, 0:n, 0:D], NE, 2), MUL).then_inc(fprod_ready, 1)
            pool.wait_ge(fp_ready, 1)
            for s in (4, 3):
                gate_products(G, s).then_inc(gprod_ready, 1)
            pool.wait_ge(pc_ready, 1)
            for t in (2, 3, 4):
                last = mixed_products(G, t)
            last.then_inc(mixp_ready, 1)

            attention(2, h)

        @block.tensor
        def _(pe):
            def mm(o, lhsT, rhs, start=True, stop=True, **k):
                return nc.tensor.matmul(o, lhsT, rhs, start=start, stop=stop, **k)

            def keep_warm(n):
                for _ in range(n):
                    mm(bank[7][:, :], idle[:, 0:128], idle[:, :])

            def turn(k, src, wait_lo, n_lo, wait_hi, n_hi, hi_first=False):
                for lo in ((False, True) if hi_first else (True, False)):
                    pe.wait_ge(*((wait_lo, n_lo) if lo else (wait_hi, n_hi)))
                    for s in range(S)[LO if lo else HI]:
                        o = bank[1][0:D, s * B:(s + 1) * B] if lo else bank[2][0:D, (s - S0) * B:(s - S0 + 1) * B]
                        last = nc.tensor.transpose(o, src[:, s, :], ident[:, :])
                    last.then_inc(turned_lo if lo else turned_hi, 1)

            def attention(k, w, extra):
                pe.wait_ge(aT_hi, [0, 1, 5][k])
                for s in range(S0, S):
                    last = mm(bank[4][:, (s - S0) * D:(s - S0 + 1) * D], aT[0:D, s, :], w[:, 0:D])
                last.then_inc(q_hi_mm, 1)
                pe.wait_ge(aT_lo, [0, 1, 5][k])
                for s in range(S0):
                    last = mm(bank[3][:, s * D:(s + 1) * D], aT[0:D, s, :], w[:, 0:D])
                last.then_inc(q_lo_mm, 1)
                n = D + extra
                for s in range(S):
                    last = mm(bank[5][:, s * n:(s + 1) * n], aT[0:D, s, :], w[:, D:D + n])
                last.then_inc(v_mm, 1)

            pe.wait_ge(idle_ready, 1)
            keep_warm(7)

            h_ps = bank[0]
            centre = part(wa_sb, WA, "centre")
            pe.wait_ge(wt_in[0], 16)
            chunk = {a: m for m, (a, _) in enumerate(XCHUNKS)}
            for q in range(PAIRS):
                m, j = divmod(q, STEPS)
                if q in chunk:
                    pe.wait_ge(x_in[chunk[q]], 16)
                if q == 2:
                    pe.wait_ge(wt_in[1], 16)
                lo = m - 2 if j == 0 else m - 1
                w0 = 0 if j == 0 else D + 2 * D * j
                if lo < 0:
                    w0 -= lo * D
                    lo = 0
                hi = min(m, S - 1)
                mm(h_ps[:, lo * D:(hi + 1) * D], x_sb[:, q, :], wt_sb[:, w0:w0 + (hi + 1 - lo) * D],
                   start=(q == 0), stop=False, skip_group_check=True)
                if q == 18:
                    pe.wait_ge(wa_in, 16)
                    mm(bank[3][0:D, 0:D], part(wa_sb, WA, "q"), part(wa_sb, WA, "k")).then_inc(prep_mm, 1)
                if q == 24:
                    pe.wait_ge(prep_cp, 1)
                    mm(bank[3][0:D, 0:D], a0_t1[:, :], centre).then_inc(prep_mm, 1)
                if q == 30:
                    pe.wait_ge(prep_cp, 2)
                    mm(bank[3][0:D, 0:D], a0_u[:, :], centre)
                    mm(bank[3][0:D, D:2 * D], centre, part(wa_sb, WA, "v")).then_inc(prep_mm, 1)
            pe.wait_ge(tokb_in, 16)
            mm(h_ps[:, 0:S * D], part(tokb_sb, TOKB, "ones"), part(tokb_sb, TOKB, "tok_b"), start=False,
               skip_group_check=True).then_inc(tok_done, 1)
            keep_warm(3)

            pe.wait_ge(ident_in_s, 16)
            turn(1, h, h_ready, 1, h_ready, 1, hi_first=True)
            keep_warm(2)
            pe.wait_ge(prep_cp, 3)
            attention(1, a0_w, 0)

            pe.wait_ge(wb_in, 16)
            mm(bank[6][0:D, 0:NE * NC], part(wb_sb, WB, "bd_vt", D), part(wb_sb, WB, "bd_g", D))
            for e in range(NE):
                a = WB["bd_q"][0] + e * D
                last = mm(bank[6][0:D, NE * NC + e * D:NE * NC + (e + 1) * D], wb_sb[0:D, a:a + D],
                          part(wb_sb, WB, "bd_k", D))
            last.then_inc(prep_mm, 1)
            pe.wait_ge(wc_in, 16)
            c_q, c_k = part(wc_sb, WC, "q", D), part(wc_sb, WC, "k", D)
            c_bk, c_bq = part(wc_sb, WC, "bk", D), part(wc_sb, WC, "bq", D)
            mm(bank[0][0:D, 0:D], c_q, c_k)
            mm(bank[0][0:D, D:2 * D], part(wc_sb, WC, "v", D), part(wc_sb, WC, "o_t", D))
            mm(bank[0][0:D, 2 * D:2 * D + 1], c_q, c_bk)
            mm(bank[0][0:D, 2 * D + 1:2 * D + 2], c_k, c_bq)
            mm(bank[0][:, 192:193], c_bq.broadcast_to([D, B]), c_bk)
            mm(bank[0][:, 193:193 + D], part(wc_sb, WC, "bv", D).broadcast_to([D, B]), part(wc_sb, WC, "o_t", D),
               stop=False)
            mm(bank[0][:, 193:193 + D], part(wc_sb, WC, "ones", 1), part(wc_sb, WC, "bo", 1), start=False)
            mm(bank[0][:, 300:300 + NH], part(wb_sb, WB, "fn_b", D).broadcast_to([D, B]),
               part(wb_sb, WB, "fg_t", D)).then_inc(prep_mm, 1)
            keep_warm(8)
            pe.wait_ge(prep_cp, 4)
            mm(bank[6][0:D + 1, 0:D + NE * NC + NE * D], part(wb_sb, WB, "hl_t", D), f_r[:, :]).then_inc(prep_mm, 1)
            pe.wait_ge(prep_cp, 5)
            mm(bank[0][0:D, 0:D], a1_t1[:, :], centre)
            mm(bank[0][0:D, D:2 * D + 2], centre, a1_y[:, :]).then_inc(prep_mm, 1)
            keep_warm(8)
            pe.wait_ge(prep_cp, 7)
            mm(bank[0][0:D, 0:D], a1_u[:, :], centre).then_inc(prep_mm, 1)
            keep_warm(14)

            turn(2, xa, xa_lo, 1, xa_hi, 1)
            keep_warm(1)
            pe.wait_ge(prep_cp, 6)
            pe.wait_ge(aT_lo, 2)
            for s in range(S):
                if s == S0:
                    pe.wait_ge(aT_hi, 2)
                last = mm(bank[3 + s // 2][:, (s % 2) * FW:(s % 2 + 1) * FW], aT[:, s, :], wf[:, 0:FW])
                if s in (1, 3, 4):
                    last.then_inc(sxv_mm, 1)
            for s, o in ((4, bank[6][:, 0:NE * D]), (0, bank[0][:, 0:NE * D]), (1, bank[0][:, NE * D:2 * NE * D]),
                         (3, bank[1][:, 0:NE * D]), (2, bank[2][:, 0:NE * D])):
                if s == 0:
                    pe.wait_ge(prep_cp, 8)
                mm(o, aT[:, s, :], wf[:, FW:]).then_inc(fq_mm, 1)
            pe.wait_ge(sxv_act, 2)
            pe.wait_ge(sxv_dve, 1)
            pe.wait_ge(onehot_in, 16)
            for n in range(NH):
                last = mm(bank[5][:, n * S * DH:(n + 1) * S * DH], onehot_sb[:, n, :],
                          sxv[0:NH, :, n * DH:(n + 1) * DH])
            last.then_inc(resid_mm, 1)
            pe.wait_ge(pads_ready, 1)
            mm(bank[4][0:1, 0:1], pads[:, :], ones_col[:, :]).then_inc(pads_mm, 1)
            keep_warm(12)
            xh_s = xh[:, :, :].rearrange("b (s n) d -> b s (n d)", n=NH)
            turn(3, xh_s, xa_lo, 2, xa_lo, 2)
            keep_warm(1)
            fc1, fc2 = part(wb_sb, WB, "fc1"), part(wb_sb, WB, "fc2")
            pe.wait_ge(aT_lo, 3)
            mm(bank[3][0:D, 0:S0 * B], fc1, aT[:, LO, :]).then_inc(fc1_ready, 1)
            pe.wait_ge(aT_hi, 3)
            mm(bank[4][0:D, 0:S1 * B], fc1, aT[:, HI, :]).then_inc(fc1_ready, 1)
            for s in range(S):
                if s in (0, S0):
                    pe.wait_ge(hT_ready, 1 if s == 0 else 2)
                mm(bank[5][:, s * D:(s + 1) * D], aT[0:D, s, :], ident[0:D, 0:D], stop=False)
                last = mm(bank[5][:, s * D:(s + 1) * D], hT[:, s, :], fc2, start=False)
            last.then_inc(fc2_ready, 1)
            keep_warm(4)
            yc_s = yc[:, :, :].rearrange("b (s n) d -> b s (n d)", n=NH)
            turn(4, yc_s, yc_ready, 1, yc_ready, 1)
            keep_warm(1)
            pe.wait_ge(aT_lo, 4)
            for s in range(S):
                if s == S0:
                    pe.wait_ge(aT_hi, 4)
                last = mm(bank[0][:, s * NC:(s + 1) * NC], aT[0:D, s, :], fgw[:, :])
            last.then_inc(fgl_mm, 1)
            keep_warm(16)

            turn(5, h, h_ready, 3, h_ready, 3, hi_first=True)
            keep_warm(2)
            attention(2, a1_w, 2)
            keep_warm(40)

            turn(6, xa, xa_lo, 3, xa_hi, 2)
            keep_warm(1)
            w1 = WC["w1"][0]
            pe.wait_ge(aT_lo, 6)
            for c in range(KC):
                mm(bank[3 + c][:, 0:S0 * B], wc_sb[:, w1 + c * 128:w1 + (c + 1) * 128], aT[:, LO, :]).then_inc(w1_ready, 1)
            pe.wait_ge(aT_hi, 6)
            for c in range(KC):
                mm(bank[5 + c][:, 0:S1 * B], wc_sb[:, w1 + c * 128:w1 + (c + 1) * 128], aT[:, HI, :]).then_inc(w1_ready, 1)
            pe.wait_ge(rows_in, 16)
            wg = ROWS["wg"][0]
            for s in range(S):
                if s in (0, S0):
                    pe.wait_ge(gT_ready, 2 if s == 0 else 4)
                for c in range(KC):
                    last = mm(bank[0][:, s * E:(s + 1) * E], gT[:, c, s, :], rows_sb[:, wg + c * E:wg + (c + 1) * E],
                              start=(c == 0), stop=(c == KC - 1))
            last.then_inc(mlog_ready, 1)
            pe.wait_ge(wd_in, 16)
            for s in range(S):
                for c in range(KC):
                    last = mm(bank[1 + s][:, :], gT[:, c, s, :], wd_sb[:, c, :], start=(c == 0), stop=(c == KC - 1))
                last.then_inc(y_ready, 1)
                if s == 2:
                    pe.wait_ge(wsel_ready, 1)
                    nc.tensor.transpose(bank[6][0:S * E, 320:320 + B], wsel[:, :, :].rearrange("b s e -> b (s e)"),
                                        ident[:, :]).then_inc(wsel_turned, 1)
                if s == 3:
                    pe.wait_ge(wselT_ready, 1)
                    pe.wait_ge(bd_in, 16)
                    mm(bank[7][:, 0:S * D], ident[:, :], h[:, :, :], stop=False)
                    mm(bank[7][:, 0:S * D], wselT[:, :], bd_sb[:, :], start=False).then_inc(base_ready, 1)

        @block.scalar
        def _(act):
            A = nc.scalar
            steps = [0]

            def inverse_std(k, out_, tmp, var, scale, eps):
                act.wait_ge(var_ready, k)
                A.activation(tmp, var, ACT.Ln, bias=eps[:, :], scale=scale).then_inc(act_step, 1)
                steps[0] += 1
                act.wait_ge(act_step, steps[0])
                A.activation(out_, tmp, ACT.Exp, scale=-0.5).then_inc(rstd_ready, 1)

            def evacuate(lo, k, g=None, b=None):
                act.wait_ge(turned_lo if lo else turned_hi, k)
                n = S0 if lo else S1
                src = bank[1 if lo else 2][0:D, 0:n * B].rearrange("d (s b) -> d s b", b=B)
                dst = aT[0:D, LO if lo else HI, :]
                if g is None:
                    A.copy(dst, src).then_inc(aT_lo if lo else aT_hi, 1)
                else:
                    A.activation(dst, src, ACT.Identity, scale=g, bias=b).then_inc(aT_lo if lo else aT_hi, 1)

            def exponent(k, out_, in_, scale=1.0):
                act.wait_ge(sc_ready, k)
                A.activation(out_, in_, ACT.Exp, scale=scale).then_inc(exp_ready, 1)

            def attention(k, k_var, extra):
                evacuate(False, [0, 1, 5][k])
                evacuate(True, [0, 1, 5][k])
                act.wait_ge(q_hi_mm, k)
                A.copy(q_hi[:, :, :], bank[4][:, 0:S1 * D].rearrange("b (s d) -> b s d", d=D)).then_inc(q_hi_ready, 1)
                inverse_std(k_var, rstd[:, :], lnv[:, :], ag[:, :, 1], 1.0, c_eps)
                act.wait_ge(rstd_ready, k_var)
                act.wait_ge(v_mm, k)
                n = D + extra
                if extra:
                    A.copy(ab_sb[:, :, :], bank[5][:, 0:S * n].rearrange("b (s c) -> b s c", c=n)[:, :, D:n]
                           ).then_inc(v_ab, 1)
                for s in range(S):
                    last = A.activation(v_sb[:, s, :], bank[5][:, s * n:s * n + D], ACT.Copy, scale=rstd[:, s:s + 1])
                last.then_inc(v_ready, 1)

            A.preload_act_table_set("gelu_and_others")
            act.wait_ge(prep_mm, 1)
            A.copy(a0_t1[:, :], bank[3][0:D, 0:D]).then_inc(prep_cp, 1)
            act.wait_ge(prep_mm, 2)
            A.copy(a0_u[:, :], bank[3][0:D, 0:D]).then_inc(prep_cp, 1)
            act.wait_ge(prep_mm, 3)
            A.copy(a0_w[:, :], bank[3][0:D, 0:2 * D]).then_inc(prep_cp, 1)

            act.wait_ge(tok_done, 1)
            A.activation(h[:, :, :], bank[0][:, 0:S * D].rearrange("b (s d) -> b s d", d=D), ACT.Gelu).then_inc(h_ready, 1)

            act.wait_ge(turned_hi, 1)
            A.preload_act_table_set("natural_log_exp_and_others")
            attention(1, 1, 0)
            act.wait_ge(prep_mm, 4)
            A.copy(f_r[:, D:], bank[6][0:D, 0:NE * NC + NE * D])
            A.copy(f_r[:, 0:D], part(wb_sb, WB, "bd_v", D)).then_inc(prep_cp, 1)
            exponent(1, p[:, :, :], sc[:, :, :])
            act.wait_ge(prep_mm, 5)
            A.copy(a1_t1[:, :], bank[0][0:D, 0:D])
            A.copy(a1_y[:, :], bank[0][0:D, D:2 * D + 2])
            A.copy(a1_c[:, :], bank[0][:, 192:193 + D])
            A.copy(fgc[:, :], bank[0][:, 300:300 + NH]).then_inc(prep_cp, 1)
            act.wait_ge(prep_mm, 6)
            A.copy(wf[:, D:], bank[6][0:D + 1, 0:D + NE * NC + NE * D])
            A.copy(wf[:, 0:D], part(wb_sb, WB, "hl")).then_inc(prep_cp, 1)
            act.wait_ge(prep_mm, 7)
            A.copy(a1_w[:, D:], bank[0][0:D, D:2 * D + 2])
            A.copy(a1_u[:, :], bank[0][0:D, 0:D]).then_inc(prep_cp, 1)
            act.wait_ge(prep_mm, 8)
            A.copy(a1_w[:, 0:D], bank[0][0:D, 0:D])
            A.activation(fgw[:, :], part(wb_sb, WB, "fg_block", D), ACT.Copy,
                         scale=part(wb_sb, WB, "fn_g", D)).then_inc(prep_cp, 1)

            inverse_std(2, rstd[:, :], lnv[:, :], ag[:, :, 1], 1.0, c_eps)
            evacuate(True, 2)
            act.wait_ge(sxv_mm, 2)
            A.copy(sxv[:, 2:4, :], bank[4][:, 0:2 * FW].rearrange("b (s c) -> b s c", c=FW)).then_inc(sxv_act, 1)
            act.wait_ge(sxv_mm, 3)
            A.copy(sxv[:, 4, :], bank[5][:, 0:FW]).then_inc(sxv_act, 1)
            act.wait_ge(fq_mm, 1)
            A.copy(fq_hi[:, 1, :], bank[6][:, 0:NE * D]).then_inc(fq_ready, 1)
            act.wait_ge(fq_mm, 4)
            A.copy(fq_hi[:, 0, :], bank[1][:, 0:NE * D]).then_inc(fq_ready, 1)
            act.wait_ge(resid_mm, 1)
            for n in range(NH):
                last = A.copy(mixp[:, :, 0, n * DH:(n + 1) * DH],
                              bank[5][:, n * S * DH:(n + 1) * S * DH].rearrange("b (s d) -> b s d", d=DH))
            last.then_inc(resid_ready, 1)
            exponent(2, fp[:, :, :, :], fs[:, :, :, :], scale=float(DH) ** 0.5)
            exponent(3, gs[:, :, :], lb[:, :, :])
            inverse_std(3, rs[:, :], ls[:, :], s2[:, :], 1.0 / DH, c_epsf)
            evacuate(True, 3, part(wb_sb, WB, "ln_g", D), part(wb_sb, WB, "ln_b", D))
            evacuate(False, 3, part(wb_sb, WB, "ln_g", D), part(wb_sb, WB, "ln_b", D))
            evacuate(True, 4)
            evacuate(False, 4)
            inverse_std(4, rs[:, :], ls[:, :], s2[:, :], 1.0 / DH, c_epsf)
            exponent(4, fge[:, :, :], fg[:, :, :])

            attention(2, 5, 2)
            exponent(5, p[:, :, :], sc[:, :, :], scale=float(D) ** -0.5)

            inverse_std(6, rstd[:, :], lnv[:, :], ag[:, :, 1], 1.0, c_eps)
            act.wait_ge(rstd_ready, 6)
            A.preload_act_table_set("gelu_and_others")
            evacuate(True, 6)
            for c in range(KC):
                act.wait_ge(w1_ready, 1 + c)
                A.activation(gT[:, c, LO, :], bank[3 + c][:, 0:S0 * B].rearrange("p (s b) -> p s b", b=B),
                             ACT.Gelu).then_inc(gT_ready, 1)
            for c in range(KC):
                act.wait_ge(w1_ready, 3 + c)
                A.activation(gT[:, c, HI, :], bank[5 + c][:, 0:S1 * B].rearrange("p (s b) -> p s b", b=B),
                             ACT.Gelu).then_inc(gT_ready, 1)
            act.wait_ge(gT_ready, 4)
            A.preload_act_table_set("natural_log_exp_and_others")
            exponent(6, me[:, :, :], mt[:, :, :])
            act.wait_ge(wsel_turned, 1)
            A.copy(wselT[:, :], bank[6][0:S * E, 320:320 + B]).then_inc(wselT_ready, 1)

        @block.vector
        def _(dve):
            V = nc.vector
            MUL, ADD, SUB = ALU.mult, ALU.add, ALU.subtract
            steps = [0]

            def step(ins):
                steps[0] += 1
                ins.then_inc(dve_step, 1)
                return steps[0]

            def done(n):
                dve.wait_ge(dve_step, n)

            def link(ins):
                done(step(ins))

            V.memset(idle[:, :], 0.0).then_inc(idle_ready, 1)
            V.memset(aT[D:D + 1, :, :], 1.0)
            V.memset(hT[D:D + 1, :, :], 1.0)
            V.memset(fs[:, :, :, :], -1e30)
            V.memset(ones_col[:, :], 1.0)
            V.memset(c_eps[:, :], EPS)
            link(V.memset(c_epsf[:, :], EPS_FFN))

            def statistics(k_var, halves=((0, S),)):
                for s in range(S):
                    last = V.bn_stats(st[:, s, :], h[:, s, :])
                link(last)
                for s in range(S):
                    last = V.bn_aggr(ag[:, s, :], st[:, s, :])
                last.then_inc(var_ready, 1)
                dve.wait_ge(var_ready, k_var)

            def normalise(k_var):
                statistics(k_var)
                link(V.tensor_tensor(xc[:, :, :], h[:, :, :], over(ag[:, :, 0], D, 2), SUB))
                dve.wait_ge(rstd_ready, k_var)
                V.tensor_tensor(xa[:, LO, :], xc[:, LO, :], over(rstd[:, LO], D, 2), MUL).then_inc(xa_lo, 1)
                V.tensor_tensor(xa[:, HI, :], xc[:, HI, :], over(rstd[:, HI], D, 2), MUL).then_inc(xa_hi, 1)

            def evacuate_hi(k):
                dve.wait_ge(turned_hi, k)
                V.tensor_copy(aT[0:D, HI, :], bank[2][0:D, 0:S1 * B].rearrange("d (s b) -> d s b", b=B)
                              ).then_inc(aT_hi, 1)

            def attention(k, k_var, k_exp, residual):
                statistics(k_var)
                dve.wait_ge(q_lo_mm, k)
                link(V.tensor_tensor(prod[:, LO, :, :],
                                     over(bank[3][:, 0:S0 * D].rearrange("b (s d) -> b s d", d=D), S, 2),
                                     over(h[:, :, :], S0, 1), MUL))
                n_lo = step(V.tensor_reduce(sc[:, LO, :], prod[:, LO, :, :], X, ADD))
                dve.wait_ge(rstd_ready, k_var)
                n_rr = step(V.tensor_tensor(rr[:, :, :], over(rstd[:, :], S, 2), over(rstd[:, :], S, 1), MUL))
                if k == 2:
                    dve.wait_ge(v_ab, 1)
                    n = step(V.tensor_tensor(ab[:, :], ab_sb[:, :, 0], rstd[:, :], MUL))
                    n2 = step(V.tensor_tensor(ab2[:, :], ab_sb[:, :, 1], rstd[:, :], MUL))
                    done(n)
                    link(V.tensor_scalar(ab[:, :], ab[:, :], a1_c[:, 0:1], None, ADD))
                    n_rr = step(V.tensor_tensor(abst[:, :, :], over(ab[:, :], S, 2), over(ab2[:, :], S, 1), ADD))
                dve.wait_ge(sprod_hi, k)
                link(V.tensor_reduce(sc[:, HI, :], prod[:, HI, :, :], X, ADD))
                link(V.tensor_tensor(sc[:, :, :], sc[:, :, :], rr[:, :, :], MUL))
                if k == 2:
                    link(V.tensor_tensor(sc[:, :, :], sc[:, :, :], abst[:, :, :], ADD))
                link(V.tensor_reduce(mx[:, :], sc[:, :, :], X, ALU.max))
                V.tensor_tensor(sc[:, :, :], sc[:, :, :], over(mx[:, :], S, 2), SUB).then_inc(sc_ready, 1)
                dve.wait_ge(exp_ready, k_exp)
                link(V.tensor_reduce(sm[:, :], p[:, :, :], X, ADD))
                link(V.reciprocal(sm[:, :], sm[:, :]))
                scale = float(D) ** -0.5 if k == 1 else 1.0
                V.scalar_tensor_tensor(p[:, :, :], p[:, :, :], scale, over(sm[:, :], S, 2), MUL, MUL).then_inc(p_ready, 1)
                dve.wait_ge(p_ready, k)
                dve.wait_ge(v_ready, k)
                link(V.tensor_tensor(pvp[:, LO, :, :], over(v_sb[:, :, :], S0, 1), over(p[:, LO, :], D, 3), MUL))
                link(V.tensor_reduce(att[:, LO, :], pvp[:, LO, :, :].rearrange("b s t d -> b s d t"), X, ADD))
                dve.wait_ge(pvp_hi, k)
                link(V.tensor_reduce(att[:, HI, :], pvp[:, HI, :, :].rearrange("b s t d -> b s d t"), X, ADD))
                return V.tensor_tensor(h[:, :, :], residual[:, :, :], att[:, :, :], ADD)

            def inner_statistics(yc_sem=None):
                link(V.tensor_reduce(s1[:, :], y[:, :, :], X, ADD))
                c = V.scalar_tensor_tensor(yc[:, :, :], over(s1[:, :], DH, 2), -1.0 / DH, y[:, :, :], MUL, ADD)
                if yc_sem is not None:
                    c.then_inc(yc_sem, 1)
                    dve.wait_ge(yc_sem, 1)
                else:
                    link(c)
                link(V.tensor_tensor(sq[:, :, :], yc[:, :, :], yc[:, :, :], MUL))
                V.tensor_reduce(s2[:, :], sq[:, :, :], X, ADD).then_inc(var_ready, 1)

            dve.wait_ge(h_ready, 1)
            attention(1, 1, 1, h).then_inc(h_ready, 1)
            dve.wait_ge(h_ready, 2)

            normalise(2)
            evacuate_hi(2)
            dve.wait_ge(sxv_mm, 1)
            V.tensor_copy(sxv[:, 0:2, :], bank[3][:, 0:2 * FW].rearrange("b (s c) -> b s c", c=FW)).then_inc(sxv_dve, 1)
            dve.wait_ge(sxv_dve, 1)
            q4 = {0: bank[0][:, 0:NE * D], 1: bank[0][:, NE * D:2 * NE * D], 2: bank[2][:, 0:NE * D]}
            order = {0: 3, 1: 3, 2: 5}
            n_prod = {}
            for s in range(S0):
                dve.wait_ge(fq_mm, order[s])
                if s == 2:
                    dve.wait_ge(sxv_act, 1)
                n = s + 1
                n_prod[s] = step(V.tensor_tensor(fprod[s][:, :, :].rearrange("b t (e c) -> b t e c", e=NE),
                                                 over(q4[s].rearrange("b (e c) -> b e c", e=NE), n, 1),
                                                 over(sxv[:, 0:n, 0:D], NE, 2), MUL))
                if s == 1:
                    dve.wait_ge(sxv_act, 2)
                    V.tensor_scalar(iszero[:, :, :], sxv[:, :, 0:D], 0.0, None, ALU.is_equal, ALU.add,
                                    accum_out=pads[:, :]).then_inc(pads_ready, 1)

            def score_sums(s):
                return V.tensor_reduce(fs[:, s, 0:s + 1, :].rearrange("b t c -> b (t c)"),
                                       fprod[s][:, :, :].rearrange("b t (c d) -> b (t c) d", d=DH), X, ADD)

            for s in range(S0):
                done(n_prod[s])
                score_sums(s)
            dve.wait_ge(pads_mm, 1)
            n_pads = step(V.tensor_copy(pads_i[:, :], bank[4][0:1, 0:1]))
            for i, s in enumerate((4, 3)):
                dve.wait_ge(fprod_ready, i + 1)
                last = score_sums(s)
            link(last)
            link(V.tensor_reduce(fm[:, :, :], fs[:, :, :, :].rearrange("b s t c -> b s c t"), X, ALU.max))
            V.tensor_tensor(fs[:, :, :, :], fs[:, :, :, :], over(fm[:, :, :], S, 2), SUB).then_inc(sc_ready, 1)
            padded = ctx.enter_context(V.register("padded"))
            V.reg_load(padded, pads_i[0:1, 0:1])
            dve.wait_ge(exp_ready, 2)
            link(V.tensor_reduce(fr[:, :, :], fp[:, :, :, :].rearrange("b s t c -> b s c t"), X, ADD))
            link(V.reciprocal(fr[:, :, :], fr[:, :, :]))
            V.tensor_tensor(fp[:, :, :, :], fp[:, :, :, :], over(fr[:, :, :], S, 2), MUL).then_inc(fp_ready, 1)
            dve.wait_ge(fp_ready, 1)
            for s in range(S0):
                last = gate_products(V, s)
            link(last)

            def gate_sums(s):
                return V.tensor_reduce(lg[:, s, :], gprod[s][:, :, :, :].rearrange("b t e c -> b c (t e)"), X, ADD)

            for s in range(S0):
                gate_sums(s)
            dve.wait_ge(gprod_ready, 1)
            gate_sums(4)
            dve.wait_ge(gprod_ready, 2)
            link(gate_sums(3))

            with V.If_ne(padded, 0):
                fixes = [0]

                def fix(ins):
                    fixes[0] += 1
                    ins.then_inc(fix_step, 1)
                    dve.wait_ge(fix_step, fixes[0])

                dve.wait_ge(gate_rows_in, 16)
                fix(V.tensor_scalar(fix_np[:, :, :], sxv[:, :, 0:D], 0.0, None, ALU.not_equal))
                for s in range(S):
                    n = s + 1
                    for t in range(n):
                        v4 = sxv[:, t, D:2 * D].rearrange("b (h d) -> b h d", h=NH)
                        p4 = fp[:, s, t, :].rearrange("b (e h) -> b e h", h=NH)
                        last = V.tensor_tensor(fix_prod[:, t, :].rearrange("b (e h d) -> b e h d", e=NE, h=NH),
                                               over(v4, NE, 1), over(p4, DH, 3), MUL)
                    fix(last)
                    fix(V.tensor_reduce(fix_om[:, s, :], fix_prod[:, 0:n, :].rearrange("b t c -> b c t"), X, ADD))
                    o4 = fix_om[:, s, :].rearrange("b (e c) -> b e c", e=NE)
                    fix(V.tensor_tensor(o4, o4, over(fix_np[:, s, :], NE, 1), MUL))
                for f in range(NE):
                    fix(V.tensor_tensor(fix_prod[:, :, :], fix_om[:, :, :], over(gate_rows_sb[:, f, :], S, 1), MUL))
                    fix(V.tensor_reduce(fix_g[:, :, :], fix_prod[:, :, :].rearrange("b s (e c) -> b s c e", e=NE), X, ADD))
                    fix(V.tensor_reduce(lg[:, :, f * NH:(f + 1) * NH],
                                        fix_g[:, :, :].rearrange("b s (h d) -> b s h d", h=NH), X, ADD))
            dve.wait_ge(rows_in, 16)
            link(V.tensor_tensor(lb[:, :, :], lg[:, :, :], over(part(rows_sb, ROWS, "gate_b"), S, 1), ADD))

            def by_gate(t):
                return t[:, :, :].rearrange("b s (e h) -> b s e h", h=NH)

            link(V.tensor_reduce(gm[:, :, :], lb[:, :, :].rearrange("b s (e h) -> b s h e", h=NH), X, ALU.max))
            V.tensor_tensor(by_gate(lb), by_gate(lb), over(gm[:, :, :], NE, 2), SUB).then_inc(sc_ready, 1)
            dve.wait_ge(exp_ready, 3)
            link(V.tensor_reduce(gr[:, :, :], gs[:, :, :].rearrange("b s (e h) -> b s h e", h=NH), X, ADD))
            link(V.reciprocal(gr[:, :, :], gr[:, :, :]))
            link(V.tensor_tensor(by_gate(gs), by_gate(gs), over(gr[:, :, :], NE, 2), MUL))
            link(V.tensor_tensor(pcp[:, :, :, :], fp[:, :, :, :], over(gs[:, :, :], S, 2), MUL))
            V.tensor_reduce(pc[:, :, :, :].rearrange("b s t h -> b (s t) h"),
                            pcp[:, :, :, :].rearrange("b s t (e h) -> b (s t) h e", h=NH), X, ADD).then_inc(pc_ready, 1)
            dve.wait_ge(pc_ready, 1)
            mixed_products(V, 0)
            link(mixed_products(V, 1))
            dve.wait_ge(resid_ready, 1)

            def mixed_sums(s):
                return V.tensor_reduce(y[:, s * NH:(s + 1) * NH, :].rearrange("b n d -> b (n d)"),
                                       mixp[:, s, 0:s + 2, :].rearrange("b t c -> b c t"), X, ADD)

            mixed_sums(0)
            mixed_sums(1)
            dve.wait_ge(mixp_ready, 1)
            for s in (2, 3, 4):
                last = mixed_sums(s)
            link(last)
            y_s = y[:, :, :].rearrange("b (s n) d -> b s (n d)", n=NH)
            with V.If_ne(padded, 0):
                resid = mixp[:, :, 0, :]
                fix(V.tensor_tensor(y_s, y_s, resid, SUB))
                fix(V.tensor_tensor(y_s, y_s, fix_np[:, :, :], MUL))
                fix(V.tensor_tensor(y_s, y_s, resid, ADD))
            inner_statistics()
            dve.wait_ge(rstd_ready, 3)
            V.tensor_tensor(xh[:, :, :], yc[:, :, :], over(rs[:, :], DH, 2), MUL).then_inc(xa_lo, 1)
            dve.wait_ge(xa_lo, 2)
            xh_s = xh[:, :, :].rearrange("b (s n) d -> b s (n d)", n=NH)
            link(V.tensor_tensor(f1g[:, :, :], xh_s, over(part(rows_sb, ROWS, "ln_g"), S, 1), MUL))
            link(V.tensor_tensor(f1[:, :, :], f1g[:, :, :], over(part(rows_sb, ROWS, "ln_b"), S, 1), ADD))
            n_m1 = step(V.tensor_scalar(m1[:, :, :], f1[:, :, :], 0.0, None, ALU.not_equal))
            dve.wait_ge(aT_lo, 3)
            dve.wait_ge(aT_hi, 3)
            link(V.tensor_scalar(m1T[:, :, :], aT[0:D, :, :], 0.0, None, ALU.not_equal))
            for i, (a, b, bk) in enumerate(((0, S0, 3), (S0, S, 4))):
                dve.wait_ge(fc1_ready, i + 1)
                V.scalar_tensor_tensor(hT[0:D, a:b, :], bank[bk][0:D, 0:(b - a) * B].rearrange("d (s b) -> d s b", b=B),
                                       0.0, m1T[:, a:b, :], ALU.max, MUL).then_inc(hT_ready, 1)
            dve.wait_ge(fc2_ready, 1)
            link(V.tensor_tensor(y_s, bank[5][:, 0:S * D].rearrange("b (s d) -> b s d", s=S), m1[:, :, :], MUL))
            inner_statistics(yc_ready)
            dve.wait_ge(rstd_ready, 4)
            n_xh = step(V.tensor_tensor(xh[:, :, :], yc[:, :, :], over(rs[:, :], DH, 2), MUL))
            dve.wait_ge(fgl_mm, 1)
            n_fgp = step(V.tensor_tensor(fgp[:, :, :, :],
                                         bank[0][:, 0:S * NC].rearrange("b (s f n) -> b s f n", s=S, f=NH),
                                         over(rs[:, :].rearrange("b (s n) -> b s n", n=NH), NH, 2), MUL))
            done(n_xh)
            n_fo = step(V.tensor_tensor(f1g[:, :, :], xh_s, over(part(rows_sb, ROWS, "fn_g"), S, 1), MUL))
            done(n_fgp)
            link(V.tensor_reduce(fg[:, :, :], fgp[:, :, :, :], X, ADD))
            link(V.tensor_tensor(fg[:, :, :], fg[:, :, :], over(fgc[:, :], S, 1), ADD))
            link(V.tensor_reduce(fgm[:, :], fg[:, :, :], X, ALU.max))
            V.tensor_tensor(fg[:, :, :], fg[:, :, :], over(fgm[:, :], NH, 2), SUB).then_inc(sc_ready, 1)
            n_fo = step(V.tensor_tensor(fo[:, :, :], f1g[:, :, :], over(part(rows_sb, ROWS, "fn_b"), S, 1), ADD))
            dve.wait_ge(exp_ready, 4)
            link(V.tensor_reduce(fgr[:, :], fge[:, :, :], X, ADD))
            link(V.reciprocal(fgr[:, :], fgr[:, :]))
            link(V.tensor_tensor(fge[:, :, :], fge[:, :, :], over(fgr[:, :], NH, 2), MUL))
            fo3 = fo[:, :, :].rearrange("b s (n d) -> b (s n) d", n=NH)
            link(V.tensor_tensor(yc[:, :, :], fo3, over(fge[:, :, :].rearrange("b s n -> b (s n)"), DH, 2), MUL))
            V.tensor_tensor(h[:, :, :], h[:, :, :], yc[:, :, :].rearrange("b (s n) d -> b s (n d)", n=NH), ADD
                            ).then_inc(h_ready, 1)
            dve.wait_ge(h_ready, 3)

            attention(2, 5, 5, hb).then_inc(h_ready, 1)
            dve.wait_ge(h_ready, 4)

            normalise(6)
            evacuate_hi(6)
            dve.wait_ge(mlog_ready, 1)
            link(V.tensor_tensor(ml[:, :, :], bank[0][:, 0:S * E].rearrange("b (s e) -> b s e", s=S),
                                 over(part(rows_sb, ROWS, "bg"), S, 1), ADD))
            link(V.tensor_reduce(mlm[:, :], ml[:, :, :], X, ALU.max))
            V.tensor_tensor(mt[:, :, :], ml[:, :, :], over(mlm[:, :], E, 2), SUB).then_inc(sc_ready, 1)
            dve.wait_ge(exp_ready, 6)
            link(V.tensor_reduce(mr[:, :], me[:, :, :], X, ADD))
            link(V.reciprocal(mr[:, :], mr[:, :]))
            link(V.tensor_tensor(mp[:, :, :], me[:, :, :], over(mr[:, :], E, 2), MUL))
            link(V.tensor_reduce(mlm[:, :], mp[:, :, :], X, ALU.max))
            link(V.tensor_tensor(mt[:, :, :], mp[:, :, :], over(mlm[:, :], E, 2), ALU.is_equal))
            link(V.tensor_tensor(mt[:, :, :], mt[:, :, :], over(part(rows_sb, ROWS, "first"), S, 1), MUL))
            link(V.tensor_reduce(mlm[:, :], mt[:, :, :], X, ALU.max))
            link(V.tensor_tensor(mt[:, :, :], mt[:, :, :], over(mlm[:, :], E, 2), ALU.is_equal))
            V.tensor_tensor(wsel[:, :, :], mt[:, :, :], mp[:, :, :], MUL).then_inc(wsel_ready, 1)
            dve.wait_ge(wsel_ready, 1)
            for s in range(S):
                dve.wait_ge(y_ready, s + 1)
                link(V.tensor_tensor(yprod[:, s, :, :], bank[1 + s][:, :].rearrange("b (e c) -> b e c", e=E),
                                     over(wsel[:, s, :], D, 2), MUL))
                last = V.tensor_reduce(ysum[:, s, :], yprod[:, s, :, :].rearrange("b e c -> b c e"), X, ADD)
            link(last)
            dve.wait_ge(base_ready, 1)
            V.tensor_tensor(fin[:, :, :], bank[7][:, 0:S * D].rearrange("b (s d) -> b s d", s=S), ysum[:, :, :],
                            ADD).then_inc(fin_ready, 1)


def kernel(**inputs):
    import numpy as np
    import concourse.bacc as _bacc
    from concourse import mybir as _mybir
    from concourse.bass_utils import run_bass_kernel_spmd as _run

    i = {k: np.asarray(v) for k, v in inputs.items()}
    f = np.float32
    x = i["x"][:, 0, :PH, :2 * PAIRS].reshape(B, PH, PAIRS, 2).transpose(3, 1, 2, 0).reshape(128, PAIRS, B)
    wt = i["L0_tok_weight"].reshape(PH, PW, D)
    tok = np.zeros((2, PH, D + STEPS * 2 * D), f)
    tok[0, :, 0:D] = wt[:, PW - 1]
    for j in range(STEPS):
        for c in range(2):
            a = D + 2 * D * j
            tok[c, :, a:a + D] = wt[:, SW + 2 * j + c]
            tok[c, :, a + D:a + 2 * D] = wt[:, 2 * j + c]
    tok = tok.reshape(128, -1)

    def heads(w):
        m = np.zeros((NH, w.shape[1], NH, w.shape[2]), f)
        for n in range(NH):
            m[n, :, n, :] = w[n]
        return m.reshape(NH * w.shape[1], NH * w.shape[2])

    def same(w):
        return heads(np.broadcast_to(w, (NH, DH, DH)))

    def row(a, b):
        return np.concatenate([a, b.reshape(1, -1)], axis=0)

    def pack(tab, n, rows, **blocks):
        a = np.zeros((rows, n), f)
        for name, block in blocks.items():
            block = block if block.ndim == 2 else block.reshape(-1, 1)
            a[:block.shape[0], tab[name][0]:tab[name][0] + block.shape[1]] = block
        return a

    def all_rows(v):
        return np.broadcast_to(v.reshape(1, -1), (128, v.size))

    tokb = pack(TOKB, N_TOKB, 1, tok_b=np.tile(i["L0_tok_bias"], S)[None], ones=np.ones((1, 128), f))
    wa = pack(WA, N_WA, D, q=i["L0_attn_Wq"], k=i["L0_attn_Wk"], v=i["L0_attn_Wv"].T,
              centre=(np.eye(D) - 1.0 / D).astype(f))
    hl, hb = i["L0_ffn_hl_w"].reshape(D, D), i["L0_ffn_hl_b"].reshape(-1)
    gate_w = i["L0_ffn_gate_w"].reshape(NH, NE, NE, DH)
    bd_g = np.zeros((NH, DH, NE, NE, NH), f)
    gate_rows = np.zeros((NE, NE, NH, DH), f)
    fg_block = np.zeros((NH, DH, NH, NH), f)
    fgate = i["L0_ffn_fgate_w"].reshape(NH, NH, DH)
    for n in range(NH):
        bd_g[n, :, :, :, n] = gate_w[n].transpose(2, 1, 0)
        gate_rows[:, :, n, :] = gate_w[n]
        fg_block[n, :, :, n] = fgate[:, n].T
    wv = heads(i["L0_ffn_wv"])
    wb = pack(WB, N_WB, D + 1, hl_t=np.concatenate([hl, hb[:, None]], axis=1), hl=row(hl.T, hb), bd_v=wv.T, bd_vt=wv,
              bd_g=bd_g.reshape(D, -1),
              bd_q=np.concatenate([heads(i["L0_ffn_wq"][:, e]) for e in range(NE)], axis=1),
              bd_k=heads(i["L0_ffn_wk"]),
              fc1=row(same(i["L0_ffn_fc1_w"].T), np.tile(i["L0_ffn_fc1_b"], NH)),
              fc2=row(same(i["L0_ffn_fc2_w"].T), np.tile(i["L0_ffn_fc2_b"], NH)),
              ln_g=np.tile(i["L0_ffn_ln_g"], NH), ln_b=np.tile(i["L0_ffn_ln_b"], NH),
              fn_g=np.tile(i["L0_ffn_fnorm_g"], NH), fn_b=np.tile(i["L0_ffn_fnorm_b"], NH),
              fg_block=fg_block.reshape(D, -1), fg_t=i["L0_ffn_fgate_w"].T)
    wc = pack(WC, N_WC, D + 1, q=i["L1_attn_Wq"], k=i["L1_attn_Wk"], bk=i["L1_attn_bk"], bq=i["L1_attn_bq"],
              v=i["L1_attn_Wv"], bv=i["L1_attn_bv"], o_t=i["L1_attn_Wo"].T, bo=i["L1_attn_bo"].reshape(1, -1),
              ones=np.ones((1, 128), f), w1=row(i["L1_ffn_W1"], i["L1_ffn_b1"]))
    rows = pack(ROWS, N_ROWS, 128, wg=i["L1_ffn_Wg"].reshape(KC, 128, E).transpose(1, 0, 2).reshape(128, -1),
                gate_b=all_rows(i["L0_ffn_gate_b"].T), bg=all_rows(i["L1_ffn_bg"]),
                first=all_rows(np.arange(E, 0, -1, dtype=f)),
                ln_g=all_rows(np.tile(i["L0_ffn_ln_g"], NH)), ln_b=all_rows(np.tile(i["L0_ffn_ln_b"], NH)),
                fn_g=all_rows(np.tile(i["L0_ffn_fnorm_g"], NH)), fn_b=all_rows(np.tile(i["L0_ffn_fnorm_b"], NH)))
    onehot = np.repeat(np.eye(NH, dtype=f), 128, axis=1).reshape(NH, NH, 128)
    bd = np.zeros((S, E, S, D), f)
    for s in range(S):
        bd[s, :, s, :] = i["L1_ffn_bd"]
    wd = i["L1_ffn_Wd"].transpose(1, 0, 2).reshape(KC, 128, E * D).transpose(1, 0, 2)

    nc = _bacc.Bacc("TRN2", target_bir_lowering=False, num_devices=1)
    arrays, args = {}, []
    for name, a in (("x", x), ("w_tok", tok), ("tokb", tokb), ("ident", np.eye(128, dtype=f)), ("wa", wa), ("wb", wb),
                    ("wc", wc), ("rows", rows), ("onehot", onehot), ("bd", bd.reshape(S * E, S * D)),
                    ("gate_rows", np.broadcast_to(gate_rows.reshape(1, NE, NE * D), (128, NE, NE * D))), ("wd", wd)):
        arrays[f"in_{name}"] = np.ascontiguousarray(a)
        args.append(nc.dram_tensor(f"in_{name}", a.shape, _mybir.dt.from_np(a.dtype), kind="ExternalInput").ap())
    args.append(nc.dram_tensor("out_0", (B, S, D), _mybir.dt.from_np(np.dtype(f)), kind="ExternalOutput").ap())
    vit_tower_kernel(nc, *args)
    r = _run(nc, [arrays], core_ids=[0])
    return r.results[0]["out_0"]
```

```python
import concourse.bass as bass
from concourse import mybir
from contextlib import ExitStack

B, S, D = 128, 5, 64
PH, PW, SW = 64, 25, 12
PAIRS = (SW * (S - 1) + PW + 1) // 2
STEPS = SW // 2
NH, DH, NE = 4, 16, 4
NC = NE * NH
HID, E = 256, 8
KC = HID // 128
EPS, EPS_FFN = 1e-5, 1e-8
S0 = 3
S1 = S - S0
SQ = S0 - 1
KEYS = (slice(0, S0), slice(S0, S))
WARM_GATES = 42
WN = E * D + E
VW = 2 * D + NH
FW = VW + NE * NC
HALF = E // 2 * D
WA_N = E + HALF
POOL_TOKENS, ACT_TOKEN, DVE_TOKEN = (0, 2), 3, 1
XCHUNKS = [(7, 9), (9, 12), (12, 18), (18, 24), (24, 30), (30, PAIRS), (0, 4), (4, 7)]
W_LAST = 2 * 2 * D
W_AT = [W_LAST + D, 0, 2 * D] + [W_LAST + D + 2 * D * (j - 2) for j in range(3, STEPS)]
WSPLIT = W_LAST


def table(*entries):
    at, found = 0, {}
    for name, count in entries:
        found[name] = (at, count)
        at += count
    return found, at


TOKB, N_TOKB = table(("tok_b", S * D), ("ones", 128))
WA, N_WA = table(("q", D), ("k", D), ("v", D), ("centre", D))
WB, N_WB = table(("hl_t", D + 1), ("hl", D), ("centre", D), ("mean", NH), ("bd_vt", D), ("bd_g", NE * NC), ("bd_q", NE * D),
                 ("bd_k", D), ("fc1", D), ("fc2", D), ("ln_g", 1), ("ln_b", 1), ("fn_g", 1), ("fn_b", 1),
                 ("fg_block", NH * NH), ("fg_t", NH))
WC, N_WC = table(("q", D), ("k", D), ("bk", 1), ("bq", 1), ("v", D), ("bv", 1), ("o_t", D), ("bo", D),
                 ("ones", 128), ("w1", HID))
ROWS, N_ROWS = table(("gate_b", NC), ("bg", E), ("first", E), ("ln_g", D), ("ln_b", D),
                     ("fn_g", D), ("fn_b", D))


def vit_tower_kernel(nc: bass.Bass, x: bass.AP, w_tok: bass.AP, tokb: bass.AP, ident_in: bass.AP, wa: bass.AP,
                     wb: bass.AP, wc: bass.AP, rows: bass.AP, onehot: bass.AP, bd: bass.AP, gate_rows: bass.AP,
                     wd: bass.AP, out: bass.AP):
    fp32, bf16, i32 = mybir.dt.float32, mybir.dt.bfloat16, mybir.dt.int32
    ALU = mybir.AluOpType
    ACT = mybir.ActivationFunctionType
    X = mybir.AxisListType.X

    ctx = ExitStack()
    with ctx:
        def sb(name, shape, dt=fp32):
            return ctx.enter_context(nc.sbuf_tensor(name, shape, dt))

        def sem(name):
            return ctx.enter_context(nc.semaphore(name))

        x_sb = sb("x_sb", [128, PAIRS, B])
        wt_sb = sb("wt_sb", [128, D + STEPS * 2 * D])
        tokb_sb = sb("tokb_sb", [1, N_TOKB])
        ident = sb("ident", [128, 128])
        wa_sb = sb("wa_sb", [D, N_WA])
        wb_sb = sb("wb_sb", [D + 1, N_WB])
        wc_sb = sb("wc_sb", [D + 1, N_WC])
        rows_sb = sb("rows_sb", [128, N_ROWS])
        onehot_sb = sb("onehot_sb", [NH, NH, 128])
        bd_sb = sb("bd_sb", [S * E, S * D])
        gate_rows_sb = sb("gate_rows_sb", [128, NE, NE * D])
        wd_sb = sb("wd_sb", [128, KC, WN])
        a0_t1 = sb("a0_t1", [D, D])
        a0_u = sb("a0_u", [D, D])
        a0_w = sb("a0_w", [D, 2 * D])
        f_r = sb("f_r", [D, FW - D + NE * D])
        wf = sb("wf", [D + 1, FW + NE * D + D])
        a1_t1 = sb("a1_t1", [D, D])
        a1_u = sb("a1_u", [D, D])
        a1_y = sb("a1_y", [D, D + 2])
        a1_w = sb("a1_w", [D, 2 * D + 2])
        a1_c = sb("a1_c", [B, 1 + D])
        fgw = sb("fgw", [D, NH * NH])
        idle = sb("idle", [128, 128], bf16)
        h = sb("h", [B, S, D])
        hb = sb("hb", [B, S, D])
        st = sb("st", [B, S, 6])
        ag = sb("ag", [B, S, 2])
        lnv = sb("lnv", [B, S])
        rstd = sb("rstd", [B, S])
        rr = sb("rr", [B, S, S])
        ab = sb("ab", [B, S])
        ab2 = sb("ab2", [B, S])
        abst = sb("abst", [B, S, S])
        xc = sb("xc", [B, S, D])
        xa = sb("xa", [B, S, D])
        aT = sb("aT", [D + 1, S, B])
        q_sb = sb("q_sb", [B, S - SQ, D])
        v_sb = sb("v_sb", [B, S, D])
        ab_sb = sb("ab_sb", [B, S, 2])
        prod = sb("prod", [B, S, S, D])
        pvp = sb("pvp", [B, S, S, D])
        sc = sb("sc", [B, S, S])
        mx = sb("mx", [B, S])
        p = sb("p", [B, S, S])
        sm = sb("sm", [B, S])
        att = sb("att", [B, S0, D])
        sxv = sb("sxv", [B, S, VW])
        gt = sb("gt", [B, S, NE * NC])
        sxc = sb("sxc", [NH, S, D])
        resid = sb("resid", [B, S, D])
        fq_hi = sb("fq_hi", [B, S1, NE * D])
        fprod = [sb(f"fprod{s}", [B, s + 1, NE * D]) for s in range(S)]
        fs = sb("fs", [B, S, S, NC])
        fm = sb("fm", [B, S, NC])
        fp = sb("fp", [B, S, S, NC])
        fr = sb("fr", [B, S, NC])
        iszero = sb("iszero", [B, S, D])
        pads = sb("pads", [B, 1])
        ones_col = sb("ones_col", [B, 1])
        pads_i = sb("pads_i", [1, 1], i32)
        gprod = [sb(f"gprod{s}", [B, (s + 1) * NE + 1, NC]) for s in range(S)]
        lg = sb("lg", [B, S, NC])
        lb = sb("lb", [B, S, NC])
        gm = sb("gm", [B, S, NH])
        gs = sb("gs", [B, S, NC])
        gr = sb("gr", [B, S, NH])
        pcp = sb("pcp", [B, S, S, NC])
        pc = sb("pc", [B, S, S, NH])
        mixp = sb("mixp", [B, S, S, D])
        fix_prod = sb("fix_prod", [B, S, NE * D])
        fix_om = sb("fix_om", [B, S, NE * D])
        fix_v = sb("fix_v", [B, S, D])
        fix_mix = sb("fix_mix", [B, S * NH, DH])
        fix_mean = sb("fix_mean", [B, S * NH])
        fix_g = sb("fix_g", [B, S, D])
        fix_np = sb("fix_np", [B, S, D])
        y = sb("y", [B, S * NH, DH])
        yc = sb("yc", [B, S * NH, DH])
        xh = sb("xh", [B, S * NH, DH])
        sq = sb("sq", [B, S * NH, DH])
        s1 = sb("s1", [B, S * NH])
        s2 = sb("s2", [B, S * NH])
        ls = sb("ls", [B, S * NH])
        rs = sb("rs", [B, S * NH])
        f1 = sb("f1", [B, S, D])
        f1g = sb("f1g", [B, S, D])
        m1 = sb("m1", [B, S, D])
        m1T = sb("m1T", [D, S, B])
        hT = sb("hT", [D + 1, S, B])
        fo = sb("fo", [B, S, D])
        fgp = sb("fgp", [B, S, NH, NH + 1])
        fg = sb("fg", [B, S, NH])
        fgm = sb("fgm", [B, S])
        fge = sb("fge", [B, S, NH])
        fgr = sb("fgr", [B, S])
        gT = sb("gT", [128, KC, S, B])
        mlm = sb("mlm", [B, S])
        ml = sb("ml", [B, S, E])
        me = sb("me", [B, S, E])
        mt2 = sb("mt2", [B, S, E])
        msel = sb("msel", [B, S, E])
        mcm = sb("mcm", [B, S])
        mr = sb("mr", [B, S])
        mt = sb("mt", [B, S, E])
        wsel = sb("wsel", [B, S, E])
        wselT = sb("wselT", [S * E, B])
        y_sb = sb("y_sb", [B, 2, 2, HALF])
        yprod = sb("yprod", [B, S, E, D])
        ysum = sb("ysum", [B, S, D])
        fin = sb("fin", [B, S, D])
        c_eps = sb("c_eps", [128, 1])
        c_epsf = sb("c_epsf", [128, 1])

        psum = ctx.enter_context(nc.psum_tensor("psum", [128, 8, 512], fp32))
        bank = [psum[:, i, :] for i in range(8)]

        def part(tile, tab, name, n=None):
            a, c = tab[name]
            return tile[0:n, a:a + c] if n else tile[:, a:a + c]

        wt_in = [sem("wt_in0"), sem("wt_in1")]
        x_in = [sem(f"x_in{m}") for m in range(len(XCHUNKS))]
        tokb_in = sem("tokb_in")
        ident_in_s = sem("ident_in_s")
        wa_in = sem("wa_in")
        wb_in = sem("wb_in")
        wc_in = sem("wc_in")
        rows_in = sem("rows_in")
        onehot_in = sem("onehot_in")
        bd_in = sem("bd_in")
        gate_rows_in = sem("gate_rows_in")
        wd_in = sem("wd_in")
        idle_ready = sem("idle_ready")
        tok_done = sem("tok_done")
        h_ready = sem("h_ready")
        h_lo_mm = sem("h_lo_mm")
        h_hi_mm = sem("h_hi_mm")
        h_hi_used = sem("h_hi_used")
        h_hi = sem("h_hi")
        var_ready = sem("var_ready")
        rstd_ready = sem("rstd_ready")
        xa_lo = sem("xa_lo")
        xa_hi = sem("xa_hi")
        turned_lo = sem("turned_lo")
        turned_hi = sem("turned_hi")
        aT_lo = sem("aT_lo")
        aT_hi = sem("aT_hi")
        prep_mm = sem("prep_mm")
        prep_cp = sem("prep_cp")
        qv_hi_mm = sem("qv_hi_mm")
        qv_sq_mm = sem("qv_sq_mm")
        qv_lo_mm = sem("qv_lo_mm")
        prod_lo = sem("prod_lo")
        q_hi_ready = sem("q_hi_ready")
        q_lo_ready = sem("q_lo_ready")
        v_ready = sem("v_ready")
        v_ab = sem("v_ab")
        sprod_hi = sem("sprod_hi")
        sprod_sq = sem("sprod_sq")
        hb_ready = sem("hb_ready")
        p_ready = sem("p_ready")
        pvp_lo = sem("pvp_lo")
        pvp_hi = sem("pvp_hi")
        sc_ready = sem("sc_ready")
        exp_ready = sem("exp_ready")
        sxv_mm = sem("sxv_mm")
        fq_mm = sem("fq_mm")
        sxv_act = sem("sxv_act")
        sxv_dve = sem("sxv_dve")
        fq_ready = sem("fq_ready")
        fprod_ready = sem("fprod_ready")
        pads_ready = sem("pads_ready")
        pads_mm = sem("pads_mm")
        resid_mm = sem("resid_mm")
        resid_ready = sem("resid_ready")
        fp_ready = sem("fp_ready")
        gprod_ready = sem("gprod_ready")
        pc_ready = sem("pc_ready")
        mixp_dve = sem("mixp_dve")
        mixp_pool = sem("mixp_pool")
        y_mm = sem("y_mm")
        sq_ready = sem("sq_ready")
        g_ready = sem("g_ready")
        gate_b_ready = sem("gate_b_ready")
        iszero_ready = sem("iszero_ready")
        sxc_mm = sem("sxc_mm")
        sxc_ready = sem("sxc_ready")
        yc_ready = sem("yc_ready")
        f1_ready = sem("f1_ready")
        gained = sem("gained")
        fo_ready = sem("fo_ready")
        fc1_ready = sem("fc1_ready")
        hT_ready = sem("hT_ready")
        fc2_ready = sem("fc2_ready")
        fgl_mm = sem("fgl_mm")
        w1_ready = sem("w1_ready")
        gT_ready = sem("gT_ready")
        y_first = sem("y_first")
        ml_ready = sem("ml_ready")
        y_first_in = sem("y_first_in")
        y_second_in = sem("y_second_in")
        y_pool = sem("y_pool")
        yprod_pool = sem("yprod_pool")
        y_dve = sem("y_dve")
        y_act = sem("y_act")
        y_last = sem("y_last")
        yprod_act = sem("yprod_act")
        wsel_ready = sem("wsel_ready")
        wsel_turned = sem("wsel_turned")
        wselT_ready = sem("wselT_ready")
        fin_ready = sem("fin_ready")
        out_done = [sem("out_done0"), sem("out_done1")]
        dve_step = sem("dve_step")
        act_step = sem("act_step")
        pool_step = sem("pool_step")
        fix_step = sem("fix_step")

        block = ctx.enter_context(nc.Block())

        def over(ap, n, at):
            shape = list(ap.shape)
            return ap.unsqueeze(at).broadcast_to(shape[:at] + [n] + shape[at:])

        LO, HI = slice(0, S0), slice(S0, S)

        def gate_products(engine, s):
            n = (s + 1) * NE
            return engine.tensor_tensor(gprod[s][:, 0:n, :].rearrange("b k (f h) -> b k f h", h=NH),
                                        gt[:, 0:s + 1, :].rearrange("b t (e f h) -> b (t e) f h", e=NE, h=NH),
                                        over(fp[:, s, 0:s + 1, :].rearrange("b t (e h) -> b (t e) h", h=NH), NE, 2),
                                        ALU.mult)

        def mixed_products(engine, t):
            return engine.tensor_tensor(mixp[:, t, t:S, :].rearrange("b s (n d) -> b s n d", n=NH),
                                        over(sxv[:, t, D:2 * D].rearrange("b (n d) -> b n d", n=NH), S - t, 1),
                                        over(pc[:, t:S, t, :], DH, 3), ALU.mult)

        @block.sync
        def _(sp):
            def load_x(m):
                a, b = XCHUNKS[m]
                sp.dma_start(x_sb[:, a:b, :], x[:, a:b, :]).then_inc(x_in[m], 16)

            sp.dma_start(wt_sb[:, 0:WSPLIT], w_tok[:, 0:WSPLIT]).then_inc(wt_in[0], 16)
            load_x(0)
            sp.dma_start(wt_sb[:, WSPLIT:], w_tok[:, WSPLIT:]).then_inc(wt_in[1], 16)
            load_x(1)
            load_x(2)
            sp.dma_start(wa_sb[:, :], wa).then_inc(wa_in, 16)
            for m in range(3, len(XCHUNKS)):
                load_x(m)
            sp.dma_start(ident[:, :], ident_in).then_inc(ident_in_s, 16)
            sp.dma_start(wb_sb[:, :], wb).then_inc(wb_in, 16)
            sp.dma_start(wc_sb[:, :], wc).then_inc(wc_in, 16)
            sp.dma_start(rows_sb[:, :], rows).then_inc(rows_in, 16)
            sp.dma_start(onehot_sb[:, :, :], onehot).then_inc(onehot_in, 16)
            sp.dma_start(gate_rows_sb[:, :, :], gate_rows).then_inc(gate_rows_in, 16)
            sp.dma_start(bd_sb[:, :], bd).then_inc(bd_in, 16)
            sp.dma_start(wd_sb[:, :, :], wd).then_inc(wd_in, 16)
            for i, (a, b) in enumerate(((0, S - 1), (S - 1, S))):
                sp.wait_ge(fin_ready, i + 1)
                sp.dma_start(out[:, a:b, :], fin[:, a:b, :]).then_inc(out_done[i], 16)
            for i in range(2):
                sp.wait_ge(out_done[i], 16)

        @block.gpsimd
        def _(pool):
            G = nc.gpsimd
            MUL = ALU.mult
            pool.dma_start(tokb_sb[:, :], tokb).then_inc(tokb_in, 16)

            def attention(k):
                pool.wait_ge(h_ready, 2 * k - 1)
                pool.wait_ge(q_hi_ready, k)
                for s in range(S0, S):
                    last = G.tensor_tensor(prod[:, s, :, :], over(q_sb[:, s - SQ, :], S, 1), h[:, :, :], MUL)
                last.then_inc(sprod_hi, 1)
                pool.wait_ge(q_lo_ready, k)
                G.tensor_tensor(prod[:, SQ, :, :], over(q_sb[:, 0, :], S, 1), h[:, :, :], MUL).then_inc(sprod_sq, 1)
                if k == 2:
                    G.tensor_tensor(hb[:, :, :], h[:, :, :], over(a1_c[:, 1:1 + D], S, 1), ALU.add).then_inc(hb_ready, 1)
                pool.wait_ge(v_ready, k)
                pool.wait_ge(p_ready, k)
                for keys in KEYS:
                    G.tensor_tensor(pvp[:, HI, keys, :], over(v_sb[:, keys, :], S1, 1), over(p[:, HI, keys], D, 3), MUL
                                    ).then_inc(pvp_hi, 1)

            attention(1)

            pool.wait_ge(rows_in, 16)
            for s in range(S):
                last = G.tensor_copy(gprod[s][:, (s + 1) * NE, :], part(rows_sb, ROWS, "gate_b"))
            last.then_inc(gate_b_ready, 1)
            pool.wait_ge(sxv_act, 2)
            pool.wait_ge(sxv_dve, 1)
            for i, s in enumerate((4, 3)):
                n = s + 1
                pool.wait_ge(fq_ready, i + 1)
                G.tensor_tensor(fprod[s][:, :, :].rearrange("b t (e c) -> b t e c", e=NE),
                                over(fq_hi[:, s - S0, :].rearrange("b (e c) -> b e c", e=NE), n, 1),
                                over(sxv[:, 0:n, 0:D], NE, 2), MUL).then_inc(fprod_ready, 1)
            G.tensor_scalar(iszero[:, :, :], sxv[:, :, 0:D], 0.0, None, ALU.is_equal).then_inc(iszero_ready, 1)
            pool.wait_ge(g_ready, 1)
            pool.wait_ge(fp_ready, 1)
            gate_products(G, 4).then_inc(gprod_ready, 1)
            pool.wait_ge(pc_ready, 1)
            for t in (2, 3, 4):
                mixed_products(G, t).then_inc(mixp_pool, 1)

            pool.wait_ge(gained, 1)
            pool.wait_ge(rstd_ready, 4)
            G.tensor_tensor(xh[:, :, :], f1g[:, :, :].rearrange("b s (n d) -> b (s n) d", n=NH),
                            over(rs[:, :], DH, 2), MUL).then_inc(pool_step, 1)
            pool.wait_ge(pool_step, 1)
            G.tensor_tensor(fo[:, :, :], xh[:, :, :].rearrange("b (s n) d -> b s (n d)", n=NH),
                            over(part(rows_sb, ROWS, "fn_b"), S, 1), ALU.add).then_inc(fo_ready, 1)

            attention(2)

            pool.wait_ge(wsel_ready, 1)
            pool.wait_ge(y_first_in, 1)
            for half in range(2):
                if half == 1:
                    pool.wait_ge(y_second_in, 1)
                e = slice(half * E // 2, (half + 1) * E // 2)
                for i, s in enumerate(POOL_TOKENS):
                    G.tensor_tensor(yprod[:, s, e, :], y_sb[:, i, half, :].rearrange("b (e c) -> b e c", c=D),
                                    over(wsel[:, s, e], D, 2), MUL).then_inc(yprod_pool, 1)

        @block.tensor
        def _(pe):
            def mm(o, lhsT, rhs, start=True, stop=True, **k):
                return nc.tensor.matmul(o, lhsT, rhs, start=start, stop=stop, **k)

            def keep_warm(n, spare=7):
                for _ in range(n):
                    mm(bank[spare][:, :], idle[:, :], idle[:, 0:1].broadcast_to([128, 512]))

            def turn(k, src, wait_lo, n_lo, wait_hi, n_hi, hi_first=False):
                for lo in ((False, True) if hi_first else (True, False)):
                    pe.wait_ge(*((wait_lo, n_lo) if lo else (wait_hi, n_hi)))
                    for s in range(S)[LO if lo else HI]:
                        o = bank[1][0:D, s * B:(s + 1) * B] if lo else bank[2][0:D, (s - S0) * B:(s - S0 + 1) * B]
                        last = nc.tensor.transpose(o, src[:, s, :], ident[:, :])
                    last.then_inc(turned_lo if lo else turned_hi, 1)

            def attention(k, w, extra):
                n = 2 * D + extra
                pe.wait_ge(aT_hi, [0, 1, 5][k])
                for s in range(S0, S):
                    last = mm(bank[4][:, (s - S0) * n:(s - S0 + 1) * n], aT[0:D, s, :], w[:, 0:n])
                last.then_inc(qv_hi_mm, 1)
                pe.wait_ge(aT_lo, [0, 1, 5][k])
                mm(bank[5][:, 0:n], aT[0:D, SQ, :], w[:, 0:n]).then_inc(qv_sq_mm, 1)
                for s in range(SQ):
                    last = mm(bank[3][:, s * n:(s + 1) * n], aT[0:D, s, :], w[:, 0:n])
                last.then_inc(qv_lo_mm, 1)

            def attended(k, residual):
                lo, hi = bank[1][:, 0:S0 * D], bank[2][:, 0:S1 * D]
                mm(lo, ident[:, :], residual[:, LO, :], stop=False)
                mm(hi, ident[:, :], residual[:, HI, :], stop=False)
                pe.wait_ge(pvp_lo, k)
                for t in range(S)[KEYS[1]]:
                    last = mm(lo, ident[:, :], pvp[:, LO, t, :], start=False, stop=(t == S - 1))
                last.then_inc(h_lo_mm, 1)
                for i, keys in enumerate(KEYS):
                    pe.wait_ge(pvp_hi, 2 * k - 1 + i)
                    for t in range(S)[keys]:
                        last = mm(hi, ident[:, :], pvp[:, HI, t, :], start=False, stop=(t == S - 1))
                last.then_inc(h_hi_mm, 1)

            pe.wait_ge(idle_ready, 1)
            keep_warm(7)

            h_ps = bank[0]
            centre = part(wa_sb, WA, "centre")
            pe.wait_ge(wt_in[0], 16)
            order = [q for a, b in XCHUNKS for q in range(a, b)]
            chunk = {a: m for m, (a, _) in enumerate(XCHUNKS)}
            for i, q in enumerate(order):
                m, j = divmod(q, STEPS)
                if q in chunk:
                    pe.wait_ge(x_in[chunk[q]], 16)
                if i == 2:
                    pe.wait_ge(wt_in[1], 16)
                lo = m - 2 if j == 0 else m - 1
                w0 = W_LAST if j == 0 else W_AT[j]
                if lo < 0:
                    w0 -= lo * D
                    lo = 0
                hi = min(m, S - 1)
                last = mm(h_ps[:, lo * D:(hi + 1) * D], x_sb[:, q, :], wt_sb[:, w0:w0 + (hi + 1 - lo) * D],
                          start=(i == 0), stop=(i == PAIRS - 1), skip_group_check=True)
                if i == 17:
                    pe.wait_ge(tokb_in, 16)
                    mm(h_ps[:, 0:S * D], part(tokb_sb, TOKB, "ones"), part(tokb_sb, TOKB, "tok_b"), start=False,
                       stop=False, skip_group_check=True)
                if i == 18:
                    pe.wait_ge(wa_in, 16)
                    mm(bank[3][0:D, 0:D], part(wa_sb, WA, "q"), part(wa_sb, WA, "k")).then_inc(prep_mm, 1)
                if i == 24:
                    pe.wait_ge(prep_cp, 1)
                    mm(bank[3][0:D, 0:D], a0_t1[:, :], centre).then_inc(prep_mm, 1)
                if i == 30:
                    pe.wait_ge(prep_cp, 2)
                    mm(bank[3][0:D, 0:D], a0_u[:, :], centre)
                    mm(bank[3][0:D, D:2 * D], centre, part(wa_sb, WA, "v")).then_inc(prep_mm, 1)
            last.then_inc(tok_done, 1)
            pe.wait_ge(wb_in, 16)
            vt = part(wb_sb, WB, "bd_vt", D)
            v_cols = WB["centre"][0]
            mm(bank[6][0:D, 0:D + NH], vt, wb_sb[0:D, v_cols:v_cols + D + NH])
            mm(bank[6][0:D, D + NH:FW - D], vt, part(wb_sb, WB, "bd_g", D))
            for e in range(NE):
                a = WB["bd_q"][0] + e * D
                last = mm(bank[6][0:D, FW - D + e * D:FW - D + (e + 1) * D], wb_sb[0:D, a:a + D],
                          part(wb_sb, WB, "bd_k", D))
            last.then_inc(prep_mm, 1)

            pe.wait_ge(ident_in_s, 16)
            turn(1, h, h_ready, 1, h_hi, 1, hi_first=True)
            keep_warm(1)
            pe.wait_ge(prep_cp, 3)
            attention(1, a0_w, 0)

            pe.wait_ge(prep_cp, 4)
            n = FW - D + NE * D
            mm(bank[6][0:D + 1, 0:n], part(wb_sb, WB, "hl_t", D), f_r[:, :])
            mm(bank[6][0:D + 1, n:n + D], part(wb_sb, WB, "hl_t", D), part(wb_sb, WB, "centre", D)).then_inc(prep_mm, 1)
            pe.wait_ge(wc_in, 16)
            c_q, c_k = part(wc_sb, WC, "q", D), part(wc_sb, WC, "k", D)
            c_bk, c_bq = part(wc_sb, WC, "bk", D), part(wc_sb, WC, "bq", D)
            mm(bank[0][0:D, 0:D], c_q, c_k)
            mm(bank[0][0:D, D:2 * D], part(wc_sb, WC, "v", D), part(wc_sb, WC, "o_t", D))
            mm(bank[0][0:D, 2 * D:2 * D + 1], c_q, c_bk)
            mm(bank[0][0:D, 2 * D + 1:2 * D + 2], c_k, c_bq)
            mm(bank[0][:, 192:193], c_bq.broadcast_to([D, B]), c_bk)
            mm(bank[0][:, 193:193 + D], part(wc_sb, WC, "bv", D).broadcast_to([D, B]), part(wc_sb, WC, "o_t", D),
               stop=False)
            mm(bank[0][:, 193:193 + D], part(wc_sb, WC, "ones", 1), part(wc_sb, WC, "bo", 1), start=False)
            mm(bank[0][:, 300:300 + NH], part(wb_sb, WB, "fn_b", D).broadcast_to([D, B]),
               part(wb_sb, WB, "fg_t", D)).then_inc(prep_mm, 1)
            keep_warm(2)
            pe.wait_ge(prep_cp, 6)
            mm(bank[0][0:D, 0:D], a1_t1[:, :], centre)
            mm(bank[0][0:D, D:2 * D + 2], centre, a1_y[:, :]).then_inc(prep_mm, 1)
            keep_warm(4)
            pe.wait_ge(prep_cp, 7)
            mm(bank[0][0:D, 0:D], a1_u[:, :], centre).then_inc(prep_mm, 1)
            keep_warm(1)
            attended(1, h)
            keep_warm(10)

            turn(2, xa, xa_lo, 1, xa_hi, 1)
            keep_warm(1)
            pe.wait_ge(prep_cp, 5)
            pe.wait_ge(aT_lo, 2)
            for s in range(S):
                if s == S0:
                    pe.wait_ge(aT_hi, 2)
                last = mm(bank[3 + s // 2][:, (s % 2) * FW:(s % 2 + 1) * FW], aT[:, s, :], wf[:, 0:FW])
                if s in (1, 3, 4):
                    last.then_inc(sxv_mm, 1)
            for s, o in ((4, bank[6][:, 0:NE * D]), (0, bank[0][:, 0:NE * D]), (1, bank[0][:, NE * D:2 * NE * D]),
                         (3, bank[1][:, 0:NE * D]), (2, bank[2][:, 0:NE * D])):
                if s == 0:
                    pe.wait_ge(prep_cp, 8)
                mm(o, aT[:, s, :], wf[:, FW:FW + NE * D]).then_inc(fq_mm, 1)
            for s in range(S):
                last = mm(bank[7][0:NH, s * D:(s + 1) * D], aT[:, s, 0:NH], wf[:, FW + NE * D:])
            last.then_inc(sxc_mm, 1)
            pe.wait_ge(g_ready, 1)
            keep_warm(1, spare=5)
            pe.wait_ge(sxc_ready, 1)
            pe.wait_ge(onehot_in, 16)
            y_ps = bank[5][:, 0:S * D].rearrange("b (s d) -> b s d", s=S)
            for n in range(NH):
                last = mm(y_ps[:, :, n * DH:(n + 1) * DH], onehot_sb[:, n, :], sxc[:, :, n * DH:(n + 1) * DH],
                          start=(n == 0), stop=False, skip_group_check=True)
            last.then_inc(resid_mm, 1)
            keep_warm(10)
            pe.wait_ge(pads_ready, 1)
            mm(bank[4][0:1, 0:1], pads[:, :], ones_col[:, :]).then_inc(pads_mm, 1)
            keep_warm(WARM_GATES)
            pe.wait_ge(resid_ready, 1)
            for t, ready, n in ((0, mixp_dve, 1), (2, mixp_pool, 1), (1, mixp_dve, 2), (3, mixp_pool, 2), (4, mixp_pool, 3)):
                pe.wait_ge(ready, n)
                last = mm(bank[5][:, t * D:S * D], ident[:, :], mixp[:, t, t:S, :], start=False, stop=(t == 4),
                          skip_group_check=True)
            last.then_inc(y_mm, 1)
            keep_warm(9)
            xh_s = xh[:, :, :].rearrange("b (s n) d -> b s (n d)", n=NH)
            turn(3, xh_s, xa_lo, 2, xa_hi, 2)
            keep_warm(1)
            fc1, fc2 = part(wb_sb, WB, "fc1"), part(wb_sb, WB, "fc2")
            pe.wait_ge(aT_lo, 3)
            mm(bank[3][0:D, 0:S0 * B], fc1, aT[:, LO, :]).then_inc(fc1_ready, 1)
            pe.wait_ge(aT_hi, 3)
            mm(bank[4][0:D, 0:S1 * B], fc1, aT[:, HI, :]).then_inc(fc1_ready, 1)
            pe.wait_ge(f1_ready, 1)
            for rows, bk in ((LO, 5), (HI, 6)):
                mm(bank[bk][:, 0:(rows.stop - rows.start) * D], ident[:, :], f1[:, rows, :], stop=False,
                   skip_group_check=True)
            for i, (rows, bk) in enumerate(((LO, 5), (HI, 6))):
                pe.wait_ge(hT_ready, i + 1)
                for j, s in enumerate(range(S)[rows]):
                    last = mm(bank[bk][:, j * D:(j + 1) * D], hT[:, s, :], fc2, start=False, skip_group_check=True)
                last.then_inc(fc2_ready, 1)
            keep_warm(4)
            yc_s = yc[:, :, :].rearrange("b (s n) d -> b s (n d)", n=NH)
            turn(4, yc_s, yc_ready, 1, yc_ready, 2)
            keep_warm(1)
            pe.wait_ge(aT_lo, 4)
            for s in range(S):
                if s == S0:
                    pe.wait_ge(aT_hi, 4)
                last = mm(bank[0][:, s * NC:(s + 1) * NC], aT[0:D, s, :], fgw[:, :])
            last.then_inc(fgl_mm, 1)
            keep_warm(14)

            turn(5, h, h_ready, 3, h_hi, 3, hi_first=True)
            keep_warm(1)
            attention(2, a1_w, 2)
            keep_warm(22)
            pe.wait_ge(hb_ready, 1)
            attended(2, hb)
            keep_warm(2)

            pe.wait_ge(h_ready, 4)
            pe.wait_ge(h_hi, 4)
            mm(bank[7][:, 0:S * D], ident[:, :], h[:, :, :], stop=False)
            keep_warm(2, spare=0)
            turn(6, xa, xa_lo, 3, xa_hi, 3)
            keep_warm(1, spare=0)
            w1 = WC["w1"][0]
            pe.wait_ge(aT_lo, 6)
            for c in range(KC):
                mm(bank[3 + c][:, 0:S0 * B], wc_sb[:, w1 + c * 128:w1 + (c + 1) * 128], aT[:, LO, :]).then_inc(w1_ready, 1)
            pe.wait_ge(aT_hi, 6)
            for c in range(KC):
                mm(bank[5 + c][:, 0:S1 * B], wc_sb[:, w1 + c * 128:w1 + (c + 1) * 128], aT[:, HI, :]).then_inc(w1_ready, 1)
            pe.wait_ge(wd_in, 16)

            def output(o, s, a, b, start=True):
                for c in range(KC):
                    last = mm(o, gT[:, c, s, :], wd_sb[:, c, a:b], start=(start and c == 0), stop=(c == KC - 1),
                              skip_group_check=not start)
                return last

            for s in range(S):
                if s in (0, S0):
                    pe.wait_ge(gT_ready, 2 if s == 0 else 4)
                output(bank[1 + s][:, 0:WA_N], s, 0, WA_N).then_inc(y_first, 1)
            output(bank[6][:, 0:HALF], DVE_TOKEN, WA_N, WN).then_inc(y_dve, 1)
            for i, s in enumerate(POOL_TOKENS):
                last = output(bank[0][:, i * HALF:(i + 1) * HALF], s, WA_N, WN)
            last.then_inc(y_pool, 1)
            pe.wait_ge(ml_ready, 1)
            output(bank[S][:, WA_N:WA_N + 3 * D], S - 1, WA_N, WN - D).then_inc(y_dve, 1)
            pe.wait_ge(y_first_in, 1)
            pe.wait_ge(wsel_ready, 1)
            turned_w = bank[1 + POOL_TOKENS[-1]][0:S * E, WA_N:WA_N + B]
            nc.tensor.transpose(turned_w, wsel[:, :, :].rearrange("b s e -> b (s e)"), ident[:, :]).then_inc(wsel_turned, 1)
            pe.wait_ge(yprod_act, 1)
            output(bank[1 + ACT_TOKEN][:, 0:HALF], ACT_TOKEN, WA_N, WN).then_inc(y_act, 1)
            output(bank[7][:, S * D:(S + 1) * D], S - 1, WN - D, WN, start=False)
            pe.wait_ge(wselT_ready, 1)
            pe.wait_ge(bd_in, 16)
            mm(bank[7][:, 0:S * D], wselT[:, :], bd_sb[:, :], start=False).then_inc(y_last, 1)

        @block.scalar
        def _(act):
            A = nc.scalar
            steps = [0]

            def inverse_std(k, out_, tmp, var, scale, eps):
                act.wait_ge(var_ready, k)
                A.activation(tmp, var, ACT.Ln, bias=eps[:, :], scale=scale).then_inc(act_step, 1)
                steps[0] += 1
                act.wait_ge(act_step, steps[0])
                A.activation(out_, tmp, ACT.Exp, scale=-0.5).then_inc(rstd_ready, 1)

            def evacuate(lo, k, g=None, b=None):
                act.wait_ge(turned_lo if lo else turned_hi, k)
                n = S0 if lo else S1
                src = bank[1 if lo else 2][0:D, 0:n * B].rearrange("d (s b) -> d s b", b=B)
                dst = aT[0:D, LO if lo else HI, :]
                if g is None:
                    A.copy(dst, src).then_inc(aT_lo if lo else aT_hi, 1)
                else:
                    A.activation(dst, src, ACT.Identity, scale=g, bias=b).then_inc(aT_lo if lo else aT_hi, 1)

            def exponent(k, out_, in_, scale=1.0):
                act.wait_ge(sc_ready, k)
                A.activation(out_, in_, ACT.Exp, scale=scale).then_inc(exp_ready, 1)

            def attention(k, k_var, extra):
                evacuate(False, [0, 1, 5][k])
                evacuate(True, [0, 1, 5][k])
                if k == 1:
                    act.wait_ge(prep_mm, 4)
                    A.copy(f_r[:, :], bank[6][0:D, 0:FW - D + NE * D]).then_inc(prep_cp, 1)
                n = 2 * D + extra
                hi = bank[4][:, 0:S1 * n].rearrange("b (s c) -> b s c", c=n)
                token_sq = bank[5][:, 0:n]
                lo = bank[3][:, 0:SQ * n].rearrange("b (s c) -> b s c", c=n)
                act.wait_ge(qv_hi_mm, k)
                A.copy(q_sb[:, S0 - SQ:, :], hi[:, :, 0:D]).then_inc(q_hi_ready, 1)
                act.wait_ge(qv_sq_mm, k)
                A.copy(q_sb[:, 0, :], bank[5][:, 0:D]).then_inc(q_lo_ready, 1)
                if k == 1:
                    A.preload_act_table_set("natural_log_exp_and_others")
                inverse_std(k_var, rstd[:, :], lnv[:, :], ag[:, :, 1], 1.0, c_eps)
                act.wait_ge(rstd_ready, k_var)
                for s in range(S0, S):
                    A.activation(v_sb[:, s, :], hi[:, s - S0, D:2 * D], ACT.Copy, scale=rstd[:, s:s + 1])
                if extra:
                    A.copy(ab_sb[:, HI, :], hi[:, :, 2 * D:n])
                    A.copy(ab_sb[:, SQ, :], token_sq[:, 2 * D:n])
                A.activation(v_sb[:, SQ, :], token_sq[:, D:2 * D], ACT.Copy, scale=rstd[:, SQ:SQ + 1])
                act.wait_ge(prod_lo, k)
                if extra:
                    A.copy(ab_sb[:, 0:SQ, :], lo[:, :, 2 * D:n]).then_inc(v_ab, 1)
                for s in range(SQ):
                    last = A.activation(v_sb[:, s, :], lo[:, s, D:2 * D], ACT.Copy, scale=rstd[:, s:s + 1])
                last.then_inc(v_ready, 1)

            def take_hi(k):
                act.wait_ge(h_hi_mm, k)
                act.wait_ge(h_hi_used, k)
                A.copy(h[:, HI, :], bank[2][:, 0:S1 * D].rearrange("b (s d) -> b s d", d=D)).then_inc(h_hi, 1)

            A.preload_act_table_set("gelu_and_others")
            act.wait_ge(prep_mm, 1)
            A.copy(a0_t1[:, :], bank[3][0:D, 0:D]).then_inc(prep_cp, 1)
            act.wait_ge(prep_mm, 2)
            A.copy(a0_u[:, :], bank[3][0:D, 0:D]).then_inc(prep_cp, 1)
            act.wait_ge(prep_mm, 3)
            A.copy(a0_w[:, :], bank[3][0:D, 0:2 * D]).then_inc(prep_cp, 1)

            act.wait_ge(tok_done, 1)
            for rows, ready in ((HI, h_hi), (LO, h_ready)):
                A.activation(h[:, rows, :], bank[0][:, rows.start * D:rows.stop * D].rearrange("b (s d) -> b s d", d=D),
                             ACT.Gelu).then_inc(ready, 1)

            attention(1, 1, 0)
            act.wait_ge(prep_mm, 5)
            A.copy(wf[:, D:], bank[6][0:D + 1, 0:FW + NE * D])
            A.copy(wf[:, 0:D], part(wb_sb, WB, "hl")).then_inc(prep_cp, 1)
            act.wait_ge(prep_mm, 6)
            A.copy(a1_t1[:, :], bank[0][0:D, 0:D])
            A.copy(a1_y[:, :], bank[0][0:D, D:2 * D + 2])
            A.copy(a1_c[:, :], bank[0][:, 192:193 + D])
            A.copy(fgp[:, :, :, NH], over(bank[0][:, 300:300 + NH], S, 1)).then_inc(prep_cp, 1)
            exponent(1, p[:, :, :], sc[:, :, :])
            act.wait_ge(prep_mm, 7)
            A.copy(a1_w[:, D:], bank[0][0:D, D:2 * D + 2])
            A.copy(a1_u[:, :], bank[0][0:D, 0:D]).then_inc(prep_cp, 1)
            act.wait_ge(prep_mm, 8)
            A.copy(a1_w[:, 0:D], bank[0][0:D, 0:D])
            A.activation(fgw[:, :], part(wb_sb, WB, "fg_block", D), ACT.Copy,
                         scale=part(wb_sb, WB, "fn_g", D)).then_inc(prep_cp, 1)
            take_hi(1)

            inverse_std(2, rstd[:, :], lnv[:, :], ag[:, :, 1], 1.0, c_eps)
            evacuate(True, 2)
            act.wait_ge(sxv_mm, 2)
            sxv_b4 = bank[4][:, 0:2 * FW].rearrange("b (s c) -> b s c", c=FW)
            A.copy(sxv[:, 2:4, :], sxv_b4[:, :, 0:VW]).then_inc(sxv_act, 1)
            act.wait_ge(sxv_mm, 3)
            A.copy(sxv[:, 4, :], bank[5][:, 0:VW]).then_inc(sxv_act, 1)
            act.wait_ge(fq_mm, 1)
            A.copy(fq_hi[:, 1, :], bank[6][:, 0:NE * D]).then_inc(fq_ready, 1)
            A.copy(gt[:, 2:4, :], sxv_b4[:, :, VW:FW])
            A.copy(gt[:, 4, :], bank[5][:, VW:FW])
            act.wait_ge(fq_mm, 4)
            A.copy(fq_hi[:, 0, :], bank[1][:, 0:NE * D]).then_inc(fq_ready, 1)
            act.wait_ge(sxv_dve, 1)
            A.copy(gt[:, 0:2, :], bank[3][:, 0:2 * FW].rearrange("b (s c) -> b s c", c=FW)[:, :, VW:FW]
                   ).then_inc(g_ready, 1)
            act.wait_ge(sxc_mm, 1)
            A.copy(sxc[:, :, :], bank[7][0:NH, 0:S * D].rearrange("b (s d) -> b s d", s=S)).then_inc(sxc_ready, 1)
            act.wait_ge(resid_mm, 1)
            A.copy(resid[:, :, :], bank[5][:, 0:S * D].rearrange("b (s d) -> b s d", s=S)).then_inc(resid_ready, 1)
            exponent(2, fp[:, LO, 0:S0, :], fs[:, LO, 0:S0, :], scale=float(DH) ** 0.5)
            act.wait_ge(iszero_ready, 1)
            A.activation(iszero[:, :, :], iszero[:, :, :], ACT.Copy, accum_out=pads[:, :]).then_inc(pads_ready, 1)
            exponent(3, fp[:, HI, :, :], fs[:, HI, :, :], scale=float(DH) ** 0.5)
            exponent(4, gs[:, :, :], lb[:, :, :])
            act.wait_ge(y_mm, 1)
            A.activation(sq[:, :, :], bank[5][:, 0:S * D].rearrange("b (n d) -> b n d", d=DH), ACT.Square
                         ).then_inc(sq_ready, 1)
            inverse_std(3, rs[:, :], ls[:, :], s2[:, :], 1.0 / DH, c_epsf)
            evacuate(True, 3, part(wb_sb, WB, "ln_g", D), part(wb_sb, WB, "ln_b", D))
            evacuate(False, 3, part(wb_sb, WB, "ln_g", D), part(wb_sb, WB, "ln_b", D))
            evacuate(True, 4)
            evacuate(False, 4)
            inverse_std(4, rs[:, :], ls[:, :], s2[:, :], 1.0 / DH, c_epsf)
            exponent(5, fge[:, :, :], fg[:, :, :])

            attention(2, 5, 2)
            exponent(6, p[:, :, :], sc[:, :, :], scale=float(D) ** -0.5)
            take_hi(2)

            inverse_std(6, rstd[:, :], lnv[:, :], ag[:, :, 1], 1.0, c_eps)
            act.wait_ge(rstd_ready, 6)
            A.preload_act_table_set("gelu_and_others")
            evacuate(False, 6)
            for c in range(KC):
                act.wait_ge(w1_ready, 1 + c)
                A.activation(gT[:, c, LO, :], bank[3 + c][:, 0:S0 * B].rearrange("p (s b) -> p s b", b=B),
                             ACT.Gelu).then_inc(gT_ready, 1)
            for c in range(KC):
                act.wait_ge(w1_ready, 3 + c)
                A.activation(gT[:, c, HI, :], bank[5 + c][:, 0:S1 * B].rearrange("p (s b) -> p s b", b=B),
                             ACT.Gelu).then_inc(gT_ready, 1)
            act.wait_ge(gT_ready, 4)
            A.preload_act_table_set("natural_log_exp_and_others")
            for i, s in enumerate(POOL_TOKENS):
                act.wait_ge(y_first, s + 1)
                last = A.copy(y_sb[:, i, 0, :], bank[1 + s][:, E:WA_N])
            last.then_inc(y_first_in, 1)
            exponent(7, me[:, :, :], mt[:, :, :])

            def weigh(first, src):
                for e in range(E // 2):
                    last = A.activation(yprod[:, ACT_TOKEN, first + e, :], src[:, e * D:(e + 1) * D], ACT.Copy,
                                        scale=wsel[:, ACT_TOKEN, first + e:first + e + 1])
                return last

            act.wait_ge(wsel_ready, 1)
            weigh(0, bank[1 + ACT_TOKEN][:, E:WA_N]).then_inc(yprod_act, 1)
            act.wait_ge(y_pool, 1)
            A.copy(y_sb[:, :, 1, :], bank[0][:, 0:2 * HALF].rearrange("b (s c) -> b s c", s=2)).then_inc(y_second_in, 1)
            act.wait_ge(wsel_turned, 1)
            A.copy(wselT[:, :], bank[1 + POOL_TOKENS[-1]][0:S * E, WA_N:WA_N + B]).then_inc(wselT_ready, 1)
            act.wait_ge(y_act, 1)
            weigh(E // 2, bank[1 + ACT_TOKEN][:, 0:HALF]).then_inc(yprod_act, 1)

        @block.vector
        def _(dve):
            V = nc.vector
            MUL, ADD, SUB = ALU.mult, ALU.add, ALU.subtract
            steps = [0]

            def step(ins):
                steps[0] += 1
                ins.then_inc(dve_step, 1)
                return steps[0]

            def done(n):
                dve.wait_ge(dve_step, n)

            def link(ins):
                done(step(ins))

            V.memset(idle[:, :], 0.0).then_inc(idle_ready, 1)
            V.memset(aT[D:D + 1, :, :], 1.0)
            V.memset(hT[D:D + 1, :, :], 1.0)
            V.memset(fs[:, :, :, :], -1e30)
            V.memset(ones_col[:, :], 1.0)
            V.memset(c_eps[:, :], EPS)
            link(V.memset(c_epsf[:, :], EPS_FFN))

            def statistics(k_var, k_hi=0):
                for s in range(S):
                    src = h[:, s, :]
                    if k_hi and s >= S0:
                        if s == S0:
                            dve.wait_ge(h_hi_mm, k_hi)
                        src = bank[2][:, (s - S0) * D:(s - S0 + 1) * D]
                    last = V.bn_stats(st[:, s, :], src)
                if k_hi:
                    last.then_inc(h_hi_used, 1)
                    dve.wait_ge(h_hi_used, k_hi)
                else:
                    link(last)
                for s in range(S):
                    last = V.bn_aggr(ag[:, s, :], st[:, s, :])
                last.then_inc(var_ready, 1)
                dve.wait_ge(var_ready, k_var)

            def normalise(k_var, k_hi):
                statistics(k_var, k_hi)
                dve.wait_ge(h_hi, 2 * k_hi)
                link(V.tensor_tensor(xc[:, :, :], h[:, :, :], over(ag[:, :, 0], D, 2), SUB))
                dve.wait_ge(rstd_ready, k_var)
                V.tensor_tensor(xa[:, LO, :], xc[:, LO, :], over(rstd[:, LO], D, 2), MUL).then_inc(xa_lo, 1)
                V.tensor_tensor(xa[:, HI, :], xc[:, HI, :], over(rstd[:, HI], D, 2), MUL).then_inc(xa_hi, 1)

            def evacuate(lo, k):
                dve.wait_ge(turned_lo if lo else turned_hi, k)
                n = S0 if lo else S1
                V.tensor_copy(aT[0:D, LO if lo else HI, :],
                              bank[1 if lo else 2][0:D, 0:n * B].rearrange("d (s b) -> d s b", b=B)
                              ).then_inc(aT_lo if lo else aT_hi, 1)

            def attention(k, k_var, k_exp):
                statistics(k_var)
                dve.wait_ge(qv_lo_mm, k)
                n = 2 * D if k == 1 else 2 * D + 2
                V.tensor_tensor(prod[:, 0:SQ, :, :],
                                over(bank[3][:, 0:SQ * n].rearrange("b (s c) -> b s c", c=n)[:, :, 0:D], S, 2),
                                over(h[:, :, :], SQ, 1), MUL).then_inc(prod_lo, 1)
                dve.wait_ge(prod_lo, k)
                V.tensor_reduce(sc[:, 0:SQ, :], prod[:, 0:SQ, :, :], X, ADD)
                dve.wait_ge(rstd_ready, k_var)
                step(V.tensor_tensor(rr[:, :, :], over(rstd[:, :], S, 2), over(rstd[:, :], S, 1), MUL))
                if k == 2:
                    dve.wait_ge(v_ab, 1)
                    n = step(V.tensor_tensor(ab[:, :], ab_sb[:, :, 0], rstd[:, :], MUL))
                    n2 = step(V.tensor_tensor(ab2[:, :], ab_sb[:, :, 1], rstd[:, :], MUL))
                    done(n)
                    link(V.tensor_scalar(ab[:, :], ab[:, :], a1_c[:, 0:1], None, ADD))
                    step(V.tensor_tensor(abst[:, :, :], over(ab[:, :], S, 2), over(ab2[:, :], S, 1), ADD))
                dve.wait_ge(sprod_hi, k)
                V.tensor_reduce(sc[:, HI, :], prod[:, HI, :, :], X, ADD)
                dve.wait_ge(sprod_sq, k)
                link(V.tensor_reduce(sc[:, SQ, :], prod[:, SQ, :, :], X, ADD))
                link(V.tensor_tensor(sc[:, :, :], sc[:, :, :], rr[:, :, :], MUL))
                if k == 2:
                    link(V.tensor_tensor(sc[:, :, :], sc[:, :, :], abst[:, :, :], ADD))
                link(V.tensor_reduce(mx[:, :], sc[:, :, :], X, ALU.max))
                V.tensor_tensor(sc[:, :, :], sc[:, :, :], over(mx[:, :], S, 2), SUB).then_inc(sc_ready, 1)
                dve.wait_ge(exp_ready, k_exp)
                link(V.tensor_reduce(sm[:, :], p[:, :, :], X, ADD))
                link(V.reciprocal(sm[:, :], sm[:, :]))
                scale = float(D) ** -0.5 if k == 1 else 1.0
                V.scalar_tensor_tensor(p[:, :, :], p[:, :, :], scale, over(sm[:, :], S, 2), MUL, MUL).then_inc(p_ready, 1)
                dve.wait_ge(p_ready, k)
                dve.wait_ge(v_ready, k)
                V.tensor_tensor(pvp[:, LO, KEYS[1], :], over(v_sb[:, KEYS[1], :], S0, 1), over(p[:, LO, KEYS[1]], D, 3),
                                MUL).then_inc(pvp_lo, 1)
                link(V.tensor_tensor(pvp[:, LO, KEYS[0], :], over(v_sb[:, KEYS[0], :], S0, 1),
                                     over(p[:, LO, KEYS[0]], D, 3), MUL))
                link(V.tensor_reduce(att[:, :, :], pvp[:, LO, KEYS[0], :].rearrange("b s t d -> b s d t"), X, ADD))
                dve.wait_ge(h_lo_mm, k)
                return V.tensor_tensor(h[:, LO, :], bank[1][:, 0:S0 * D].rearrange("b (s d) -> b s d", d=D),
                                       att[:, :, :], ADD)

            dve.wait_ge(h_hi, 1)
            dve.wait_ge(h_ready, 1)
            attention(1, 1, 1).then_inc(h_ready, 1)
            dve.wait_ge(h_ready, 2)

            normalise(2, 1)
            evacuate(False, 2)
            dve.wait_ge(sxv_mm, 1)
            V.tensor_copy(sxv[:, 0:2, :], bank[3][:, 0:2 * FW].rearrange("b (s c) -> b s c", c=FW)[:, :, 0:VW]
                          ).then_inc(sxv_dve, 1)
            dve.wait_ge(sxv_dve, 1)
            q4 = {0: bank[0][:, 0:NE * D], 1: bank[0][:, NE * D:2 * NE * D], 2: bank[2][:, 0:NE * D]}
            order = {0: 3, 1: 3, 2: 5}
            n_prod = {}
            for s in range(S0):
                dve.wait_ge(fq_mm, order[s])
                if s == 2:
                    dve.wait_ge(sxv_act, 1)
                n = s + 1
                n_prod[s] = step(V.tensor_tensor(fprod[s][:, :, :].rearrange("b t (e c) -> b t e c", e=NE),
                                                 over(q4[s].rearrange("b (e c) -> b e c", e=NE), n, 1),
                                                 over(sxv[:, 0:n, 0:D], NE, 2), MUL))

            def score_sums(s):
                return V.tensor_reduce(fs[:, s, 0:s + 1, :].rearrange("b t c -> b (t c)"),
                                       fprod[s][:, :, :].rearrange("b t (c d) -> b (t c) d", d=DH), X, ADD)

            blocks = ((LO, S0), (HI, S))

            def by_key(t, g):
                return t[:, blocks[g][0], 0:blocks[g][1], :].rearrange("b s t c -> b s c t")

            def key_max(g):
                return V.tensor_reduce(fm[:, blocks[g][0], :], by_key(fs, g), X, ALU.max)

            def less_max(g):
                rows, n = blocks[g]
                V.tensor_tensor(fs[:, rows, 0:n, :], fs[:, rows, 0:n, :], over(fm[:, rows, :], n, 2), SUB
                                ).then_inc(sc_ready, 1)

            def key_sum(g):
                return V.tensor_reduce(fr[:, blocks[g][0], :], by_key(fp, g), X, ADD)

            def inverse(g):
                return V.reciprocal(fr[:, blocks[g][0], :], fr[:, blocks[g][0], :])

            def normal(g):
                rows, n = blocks[g]
                return V.tensor_tensor(fp[:, rows, 0:n, :], fp[:, rows, 0:n, :], over(fr[:, rows, :], n, 2), MUL)

            def gate_sums(s):
                return V.tensor_reduce(lg[:, s, :], gprod[s][:, :, :].rearrange("b k c -> b c k"), X, ADD)

            for s in range(S0):
                done(n_prod[s])
                last = score_sums(s)
            link(last)
            n_max = step(key_max(0))
            dve.wait_ge(fprod_ready, 1)
            n_s4 = step(score_sums(4))
            done(n_max)
            less_max(0)
            dve.wait_ge(fprod_ready, 2)
            n_s3 = step(score_sums(3))
            dve.wait_ge(exp_ready, 2)
            n_sum = step(key_sum(0))
            done(n_s4)
            done(n_s3)
            n_max = step(key_max(1))
            done(n_sum)
            n_inv = step(inverse(0))
            done(n_max)
            less_max(1)
            done(n_inv)
            n_norm = step(normal(0))
            dve.wait_ge(exp_ready, 3)
            n_sum = step(key_sum(1))
            dve.wait_ge(g_ready, 1)
            done(n_norm)
            gate_products(V, 0)
            done(n_sum)
            n_inv = step(inverse(1))
            gate_products(V, 1)
            n_g = step(gate_products(V, 2))
            done(n_inv)
            normal(1).then_inc(fp_ready, 1)
            dve.wait_ge(gate_b_ready, 1)
            done(n_g)
            gate_sums(0)
            gate_sums(1)
            dve.wait_ge(fp_ready, 1)
            n_g = step(gate_products(V, 3))
            gate_sums(2)
            dve.wait_ge(pads_mm, 1)
            n_pads = step(V.tensor_copy(pads_i[:, :], bank[4][0:1, 0:1]))
            done(n_g)
            gate_sums(3)
            done(n_pads)
            padded = ctx.enter_context(V.register("padded"))
            V.reg_load(padded, pads_i[0:1, 0:1])
            dve.wait_ge(gprod_ready, 1)
            link(gate_sums(4))

            fixes = [0]

            def fix(ins):
                fixes[0] += 1
                ins.then_inc(fix_step, 1)
                dve.wait_ge(fix_step, fixes[0])

            with V.If_ne(padded, 0):
                dve.wait_ge(gate_rows_in, 16)
                fix(V.tensor_scalar(fix_np[:, :, :], sxv[:, :, 0:D], 0.0, None, ALU.not_equal))
                fix(V.tensor_tensor(fix_v[:, :, :].rearrange("b s (h d) -> b s h d", h=NH),
                                    sxv[:, :, D:2 * D].rearrange("b s (h d) -> b s h d", h=NH),
                                    over(sxv[:, :, 2 * D:VW], DH, 3), ADD))
                for s in range(S):
                    n = s + 1
                    for t in range(n):
                        v4 = fix_v[:, t, :].rearrange("b (h d) -> b h d", h=NH)
                        p4 = fp[:, s, t, :].rearrange("b (e h) -> b e h", h=NH)
                        last = V.tensor_tensor(fix_prod[:, t, :].rearrange("b (e h d) -> b e h d", e=NE, h=NH),
                                               over(v4, NE, 1), over(p4, DH, 3), MUL)
                    fix(last)
                    fix(V.tensor_reduce(fix_om[:, s, :], fix_prod[:, 0:n, :].rearrange("b t c -> b c t"), X, ADD))
                    o4 = fix_om[:, s, :].rearrange("b (e c) -> b e c", e=NE)
                    fix(V.tensor_tensor(o4, o4, over(fix_np[:, s, :], NE, 1), MUL))
                for f in range(NE):
                    fix(V.tensor_tensor(fix_prod[:, :, :], fix_om[:, :, :], over(gate_rows_sb[:, f, :], S, 1), MUL))
                    fix(V.tensor_reduce(fix_g[:, :, :], fix_prod[:, :, :].rearrange("b s (e c) -> b s c e", e=NE), X, ADD))
                    fix(V.tensor_reduce(lg[:, :, f * NH:(f + 1) * NH],
                                        fix_g[:, :, :].rearrange("b s (h d) -> b s h d", h=NH), X, ADD))
                fix(V.tensor_tensor(lg[:, :, :], lg[:, :, :], over(part(rows_sb, ROWS, "gate_b"), S, 1), ADD))

            def by_gate(t):
                return t[:, :, :].rearrange("b s (e h) -> b s e h", h=NH)

            link(V.tensor_reduce(gm[:, :, :], lg[:, :, :].rearrange("b s (e h) -> b s h e", h=NH), X, ALU.max))
            V.tensor_tensor(by_gate(lb), by_gate(lg), over(gm[:, :, :], NE, 2), SUB).then_inc(sc_ready, 1)
            dve.wait_ge(exp_ready, 4)
            link(V.tensor_reduce(gr[:, :, :], gs[:, :, :].rearrange("b s (e h) -> b s h e", h=NH), X, ADD))
            link(V.reciprocal(gr[:, :, :], gr[:, :, :]))
            link(V.tensor_tensor(by_gate(gs), by_gate(gs), over(gr[:, :, :], NE, 2), MUL))
            n_mix = []
            for rows, n in blocks:
                n_mix.append(step(V.tensor_tensor(pcp[:, rows, 0:n, :], fp[:, rows, 0:n, :], over(gs[:, rows, :], n, 2), MUL)))
            for g, (rows, n) in enumerate(blocks):
                done(n_mix[g])
                for s in range(S)[rows]:
                    last = V.tensor_reduce(pc[:, s, 0:n, :], pcp[:, s, 0:n, :].rearrange("b t (e h) -> b t h e", h=NH),
                                           X, ADD)
            last.then_inc(pc_ready, 1)
            dve.wait_ge(pc_ready, 1)
            for t in (0, 1):
                mixed_products(V, t).then_inc(mixp_dve, 1)
            dve.wait_ge(y_mm, 1)
            y_ps = bank[5][:, 0:S * D].rearrange("b (n d) -> b n d", d=DH)
            y_s = y[:, :, :].rearrange("b (s n) d -> b s (n d)", n=NH)
            with V.If_ne(padded, 0):
                g4 = gs[:, :, :].rearrange("b s (e h) -> b s e h", h=NH)
                for s in range(S):
                    last = V.tensor_tensor(fix_prod[:, s, :].rearrange("b (e h d) -> b e h d", e=NE, h=NH),
                                           fix_om[:, s, :].rearrange("b (e h d) -> b e h d", e=NE, h=NH),
                                           over(g4[:, s, :, :], DH, 3), MUL)
                fix(last)
                fix(V.tensor_reduce(fix_mix[:, :, :].rearrange("b (s h) d -> b s (h d)", s=S),
                                    fix_prod[:, :, :].rearrange("b s (e c) -> b s c e", e=NE), X, ADD))
                fix(V.tensor_reduce(fix_mean[:, :], fix_mix[:, :, :], X, ADD))
                fix(V.scalar_tensor_tensor(fix_mix[:, :, :], over(fix_mean[:, :], DH, 2), -1.0 / DH, fix_mix[:, :, :],
                                           MUL, ADD))
                fix(V.tensor_tensor(fix_mix[:, :, :], fix_mix[:, :, :],
                                    resid[:, :, :].rearrange("b s (n d) -> b (s n) d", n=NH), ADD))
                dve.wait_ge(sq_ready, 1)
                fix(V.tensor_copy(y_ps, fix_mix[:, :, :]))
                fix(V.tensor_tensor(sq[:, :, :], fix_mix[:, :, :], fix_mix[:, :, :], MUL))
            dve.wait_ge(sq_ready, 1)
            V.tensor_reduce(s2[:, :], sq[:, :, :], X, ADD).then_inc(var_ready, 1)
            dve.wait_ge(rstd_ready, 3)
            halves = (slice(0, S0 * NH), slice(S0 * NH, S * NH))
            for g, ready in zip(halves, (xa_lo, xa_hi)):
                V.tensor_tensor(xh[:, g, :], y_ps[:, g, :], over(rs[:, g], DH, 2), MUL).then_inc(ready, 1)
            dve.wait_ge(xa_lo, 2)
            dve.wait_ge(xa_hi, 2)
            xh_s = xh[:, :, :].rearrange("b (s n) d -> b s (n d)", n=NH)
            link(V.tensor_tensor(f1g[:, :, :], xh_s, over(part(rows_sb, ROWS, "ln_g"), S, 1), MUL))
            V.tensor_tensor(f1[:, :, :], f1g[:, :, :], over(part(rows_sb, ROWS, "ln_b"), S, 1), ADD).then_inc(f1_ready, 1)
            dve.wait_ge(aT_lo, 3)
            n_m1T = [step(V.tensor_scalar(m1T[:, LO, :], aT[0:D, LO, :], 0.0, None, ALU.not_equal))]
            dve.wait_ge(f1_ready, 1)
            n_m1 = step(V.tensor_scalar(m1[:, :, :], f1[:, :, :], 0.0, None, ALU.not_equal))
            dve.wait_ge(aT_hi, 3)
            n_m1T.append(step(V.tensor_scalar(m1T[:, HI, :], aT[0:D, HI, :], 0.0, None, ALU.not_equal)))
            for i, (rows, bk) in enumerate(((LO, 3), (HI, 4))):
                dve.wait_ge(fc1_ready, i + 1)
                done(n_m1T[i])
                n = rows.stop - rows.start
                V.scalar_tensor_tensor(hT[0:D, rows, :], bank[bk][0:D, 0:n * B].rearrange("d (s b) -> d s b", b=B),
                                       0.0, m1T[:, rows, :], ALU.max, MUL).then_inc(hT_ready, 1)
            n_y = []
            done(n_m1)
            for i, (rows, bk) in enumerate(((LO, 5), (HI, 6))):
                dve.wait_ge(fc2_ready, i + 1)
                n = rows.stop - rows.start
                n_y.append(step(V.tensor_tensor(y_s[:, rows, :], bank[bk][:, 0:n * D].rearrange("b (s d) -> b s d", s=n),
                                                m1[:, rows, :], MUL)))
            n_s1, n_sq = [], []
            for i, g in enumerate(halves):
                done(n_y[i])
                n_s1.append(step(V.tensor_reduce(s1[:, g], y[:, g, :], X, ADD)))
            for i, g in enumerate(halves):
                done(n_s1[i])
                V.scalar_tensor_tensor(yc[:, g, :], over(s1[:, g], DH, 2), -1.0 / DH, y[:, g, :], MUL, ADD
                                       ).then_inc(yc_ready, 1)
            for i, g in enumerate(halves):
                dve.wait_ge(yc_ready, i + 1)
                n_sq.append(step(V.tensor_tensor(sq[:, g, :], yc[:, g, :], yc[:, g, :], MUL)))
            for i, g in enumerate(halves):
                done(n_sq[i])
                last = V.tensor_reduce(s2[:, g], sq[:, g, :], X, ADD)
            last.then_inc(var_ready, 1)
            V.tensor_tensor(f1g[:, :, :], yc[:, :, :].rearrange("b (s n) d -> b s (n d)", n=NH),
                            over(part(rows_sb, ROWS, "fn_g"), S, 1), MUL).then_inc(gained, 1)
            dve.wait_ge(rstd_ready, 4)
            dve.wait_ge(fgl_mm, 1)
            n_fgp = step(V.tensor_tensor(fgp[:, :, :, 0:NH],
                                         bank[0][:, 0:S * NC].rearrange("b (s f n) -> b s f n", s=S, f=NH),
                                         over(rs[:, :].rearrange("b (s n) -> b s n", n=NH), NH, 2), MUL))
            done(n_fgp)
            link(V.tensor_reduce(fg[:, :, :], fgp[:, :, :, :], X, ADD))
            link(V.tensor_reduce(fgm[:, :], fg[:, :, :], X, ALU.max))
            V.tensor_tensor(fg[:, :, :], fg[:, :, :], over(fgm[:, :], NH, 2), SUB).then_inc(sc_ready, 1)
            dve.wait_ge(exp_ready, 5)
            link(V.tensor_reduce(fgr[:, :], fge[:, :, :], X, ADD))
            link(V.reciprocal(fgr[:, :], fgr[:, :]))
            link(V.tensor_tensor(fge[:, :, :], fge[:, :, :], over(fgr[:, :], NH, 2), MUL))
            dve.wait_ge(fo_ready, 1)
            n_out = []
            for rows, g in ((HI, halves[1]), (LO, halves[0])):
                n_out.append(step(V.tensor_tensor(yc[:, g, :], fo[:, rows, :].rearrange("b s (n d) -> b (s n) d", n=NH),
                                                  over(fge[:, rows, :].rearrange("b s n -> b (s n)"), DH, 2), MUL)))
            for n, (rows, g, ready) in zip(n_out, ((HI, halves[1], h_hi), (LO, halves[0], h_ready))):
                done(n)
                V.tensor_tensor(h[:, rows, :], h[:, rows, :], yc[:, g, :].rearrange("b (s n) d -> b s (n d)", n=NH), ADD
                                ).then_inc(ready, 1)
            dve.wait_ge(h_hi, 3)
            dve.wait_ge(h_ready, 3)

            attention(2, 5, 6).then_inc(h_ready, 1)
            dve.wait_ge(h_ready, 4)

            normalise(6, 2)
            evacuate(True, 6)
            dve.wait_ge(y_first, S)
            dve.wait_ge(y_first_in, 1)
            V.tensor_tensor(ml[:, :, :], psum[:, 1:1 + S, 0:E], over(part(rows_sb, ROWS, "bg"), S, 1), ADD
                            ).then_inc(ml_ready, 1)
            dve.wait_ge(ml_ready, 1)
            link(V.tensor_reduce(mlm[:, :], ml[:, :, :], X, ALU.max))
            V.tensor_tensor(mt[:, :, :], ml[:, :, :], over(mlm[:, :], E, 2), SUB).then_inc(sc_ready, 1)
            dve.wait_ge(sc_ready, 7)
            n_code = step(V.scalar_tensor_tensor(mt2[:, :, :], mt[:, :, :], 0.0, over(part(rows_sb, ROWS, "first"), S, 1),
                                                 ALU.is_equal, MUL))
            dve.wait_ge(exp_ready, 7)
            n_sum = step(V.tensor_reduce(mr[:, :], me[:, :, :], X, ADD))
            done(n_code)
            n_max = step(V.tensor_reduce(mcm[:, :], mt2[:, :, :], X, ALU.max))
            done(n_sum)
            n_rec = step(V.reciprocal(mr[:, :], mr[:, :]))
            done(n_max)
            n_sel = step(V.tensor_tensor(msel[:, :, :], mt2[:, :, :], over(mcm[:, :], E, 2), ALU.is_equal))
            done(n_sel)
            V.tensor_tensor(wsel[:, :, :], msel[:, :, :], over(mr[:, :], E, 2), MUL).then_inc(wsel_ready, 1)
            dve.wait_ge(wsel_ready, 1)

            def weigh(s, first, n, src):
                return step(V.tensor_tensor(yprod[:, s, first:first + n, :], src.rearrange("b (e c) -> b e c", e=n),
                                            over(wsel[:, s, first:first + n], D, 2), MUL))

            def expert_sums(s):
                return step(V.tensor_reduce(ysum[:, s, :], yprod[:, s, :, :].rearrange("b e c -> b c e"), X, ADD))

            base = bank[7][:, 0:S * D].rearrange("b (s d) -> b s d", s=S)
            weigh(DVE_TOKEN, 0, E // 2, bank[1 + DVE_TOKEN][:, E:WA_N])
            dve.wait_ge(y_dve, 1)
            n = weigh(DVE_TOKEN, E // 2, E // 2, bank[6][:, 0:HALF])
            done(n)
            expert_sums(DVE_TOKEN)
            dve.wait_ge(y_dve, 2)
            weigh(S - 1, 0, E - 1, bank[S][:, E:WN - D])
            dve.wait_ge(yprod_pool, 3)
            expert_sums(POOL_TOKENS[0])
            dve.wait_ge(yprod_pool, 4)
            expert_sums(POOL_TOKENS[1])
            dve.wait_ge(y_last, 1)
            n = weigh(S - 1, E - 1, 1, bank[7][:, S * D:(S + 1) * D])
            dve.wait_ge(yprod_act, 2)
            n_sum = expert_sums(ACT_TOKEN)
            done(n)
            n = expert_sums(S - 1)
            done(n_sum)
            V.tensor_tensor(fin[:, 0:S - 1, :], base[:, 0:S - 1, :], ysum[:, 0:S - 1, :], ADD).then_inc(fin_ready, 1)
            done(n)
            V.tensor_tensor(fin[:, S - 1, :], base[:, S - 1, :], ysum[:, S - 1, :], ADD).then_inc(fin_ready, 1)


def kernel(**inputs):
    import numpy as np
    import concourse.bacc as _bacc
    from concourse import mybir as _mybir
    from concourse.bass_utils import run_bass_kernel_spmd as _run

    i = {k: np.asarray(v) for k, v in inputs.items()}
    f = np.float32
    x = i["x"][:, 0, :PH, :2 * PAIRS].reshape(B, PH, PAIRS, 2).transpose(3, 1, 2, 0).reshape(128, PAIRS, B)
    wt = i["L0_tok_weight"].reshape(PH, PW, D)
    tok = np.zeros((2, PH, D + STEPS * 2 * D), f)
    tok[0, :, W_LAST:W_LAST + D] = wt[:, PW - 1]
    for j in range(STEPS):
        for c in range(2):
            a = W_AT[j]
            tok[c, :, a:a + D] = wt[:, SW + 2 * j + c]
            tok[c, :, a + D:a + 2 * D] = wt[:, 2 * j + c]
    tok = tok.reshape(128, -1)

    def heads(w):
        m = np.zeros((NH, w.shape[1], NH, w.shape[2]), f)
        for n in range(NH):
            m[n, :, n, :] = w[n]
        return m.reshape(NH * w.shape[1], NH * w.shape[2])

    def same(w):
        return heads(np.broadcast_to(w, (NH, DH, DH)))

    def row(a, b):
        return np.concatenate([a, b.reshape(1, -1)], axis=0)

    def pack(tab, n, rows, **blocks):
        a = np.zeros((rows, n), f)
        for name, block in blocks.items():
            block = block if block.ndim == 2 else block.reshape(-1, 1)
            a[:block.shape[0], tab[name][0]:tab[name][0] + block.shape[1]] = block
        return a

    def all_rows(v):
        return np.broadcast_to(v.reshape(1, -1), (128, v.size))

    tokb = pack(TOKB, N_TOKB, 1, tok_b=np.tile(i["L0_tok_bias"], S)[None], ones=np.ones((1, 128), f))
    wa = pack(WA, N_WA, D, q=i["L0_attn_Wq"], k=i["L0_attn_Wk"], v=i["L0_attn_Wv"].T,
              centre=(np.eye(D) - 1.0 / D).astype(f))
    hl, hb = i["L0_ffn_hl_w"].reshape(D, D), i["L0_ffn_hl_b"].reshape(-1)
    gate_w = i["L0_ffn_gate_w"].reshape(NH, NE, NE, DH)
    bd_g = np.zeros((NH, DH, NE, NE, NH), f)
    gate_rows = np.zeros((NE, NE, NH, DH), f)
    fg_block = np.zeros((NH, DH, NH, NH), f)
    fgate = i["L0_ffn_fgate_w"].reshape(NH, NH, DH)
    for n in range(NH):
        bd_g[n, :, :, :, n] = gate_w[n].transpose(2, 1, 0)
        gate_rows[:, :, n, :] = gate_w[n]
        fg_block[n, :, :, n] = fgate[:, n].T
    wv = heads(i["L0_ffn_wv"])
    wb = pack(WB, N_WB, D + 1, hl_t=np.concatenate([hl, hb[:, None]], axis=1), hl=row(hl.T, hb),
              centre=same(np.eye(DH) - 1.0 / DH), mean=np.repeat(np.eye(NH), DH, axis=0) / DH, bd_vt=wv,
              bd_g=bd_g.reshape(D, -1),
              bd_q=np.concatenate([heads(i["L0_ffn_wq"][:, e]) for e in range(NE)], axis=1),
              bd_k=heads(i["L0_ffn_wk"]),
              fc1=row(same(i["L0_ffn_fc1_w"].T), np.tile(i["L0_ffn_fc1_b"], NH)),
              fc2=row(same(i["L0_ffn_fc2_w"].T), np.tile(i["L0_ffn_fc2_b"], NH)),
              ln_g=np.tile(i["L0_ffn_ln_g"], NH), ln_b=np.tile(i["L0_ffn_ln_b"], NH),
              fn_g=np.tile(i["L0_ffn_fnorm_g"], NH), fn_b=np.tile(i["L0_ffn_fnorm_b"], NH),
              fg_block=fg_block.reshape(D, -1), fg_t=i["L0_ffn_fgate_w"].T)
    wc = pack(WC, N_WC, D + 1, q=i["L1_attn_Wq"], k=i["L1_attn_Wk"], bk=i["L1_attn_bk"], bq=i["L1_attn_bq"],
              v=i["L1_attn_Wv"], bv=i["L1_attn_bv"], o_t=i["L1_attn_Wo"].T, bo=i["L1_attn_bo"].reshape(1, -1),
              ones=np.ones((1, 128), f), w1=row(i["L1_ffn_W1"], i["L1_ffn_b1"]))
    rows = pack(ROWS, N_ROWS, 128, gate_b=all_rows(i["L0_ffn_gate_b"].T), bg=all_rows(i["L1_ffn_bg"]),
                first=all_rows(np.arange(E, 0, -1, dtype=f)),
                ln_g=all_rows(np.tile(i["L0_ffn_ln_g"], NH)), ln_b=all_rows(np.tile(i["L0_ffn_ln_b"], NH)),
                fn_g=all_rows(np.tile(i["L0_ffn_fnorm_g"], NH)), fn_b=all_rows(np.tile(i["L0_ffn_fnorm_b"], NH)))
    onehot = np.repeat(np.eye(NH, dtype=f), 128, axis=1).reshape(NH, NH, 128)
    bd = np.zeros((S, E, S, D), f)
    for s in range(S):
        bd[s, :, s, :] = i["L1_ffn_bd"]
    wd = np.concatenate([i["L1_ffn_Wg"], i["L1_ffn_Wd"].transpose(1, 0, 2).reshape(HID, E * D)], axis=1)
    wd = wd.reshape(KC, 128, WN).transpose(1, 0, 2)

    nc = _bacc.Bacc("TRN2", target_bir_lowering=False, num_devices=1)
    arrays, args = {}, []
    for name, a in (("x", x), ("w_tok", tok), ("tokb", tokb), ("ident", np.eye(128, dtype=f)), ("wa", wa), ("wb", wb),
                    ("wc", wc), ("rows", rows), ("onehot", onehot), ("bd", bd.reshape(S * E, S * D)),
                    ("gate_rows", np.broadcast_to(gate_rows.reshape(1, NE, NE * D), (128, NE, NE * D))), ("wd", wd)):
        arrays[f"in_{name}"] = np.ascontiguousarray(a)
        args.append(nc.dram_tensor(f"in_{name}", a.shape, _mybir.dt.from_np(a.dtype), kind="ExternalInput").ap())
    args.append(nc.dram_tensor("out_0", (B, S, D), _mybir.dt.from_np(np.dtype(f)), kind="ExternalOutput").ap())
    vit_tower_kernel(nc, *args)
    r = _run(nc, [arrays], core_ids=[0])
    return r.results[0]["out_0"]
```
